# Optimizing a Trainium2 kernel written in Bass

```python
import numpy as np
import jax
import jax.numpy as jnp

def _softmax(x, axis=-1):
    return jax.nn.softmax(x, axis=axis)

def _gelu(x):
    return jax.nn.gelu(x, approximate=True)

def _silu(x):
    return jax.nn.silu(x)

def _sigmoid(x):
    return jax.nn.sigmoid(x)

def _layernorm(x, axis=-1, eps=1e-05):
    m = jnp.mean(x, axis=axis, keepdims=True)
    v = jnp.var(x, axis=axis, keepdims=True)
    return (x - m) / jnp.sqrt(v + eps)

def _scatter_add(tgt, idx, src, axis=0):
    return tgt.at[idx].add(src)

def _segment_sum(src, seg, n):
    return jax.ops.segment_sum(src, seg, n)
kernel_name = 'mk_decoder_postln_d1_seqx_r4_0a7646'

def setup_inputs(seed: int=0):
    np.random.seed(seed)
    _w = jnp.asarray

    def _rec_inputs():
        import jax
        import jax.numpy as jnp
        _rk = jax.random.key(seed)
        x = 7.22e-05 + 1 * jax.random.normal(jax.random.fold_in(_rk, 1), (2, 512, 256), jnp.float32)
        _lenS = 512 - jax.random.randint(jax.random.fold_in(_rk, 7), (2,), 0, max(1, 512 // 4) + 1, jnp.int32)
        _lenS2 = 1024 - jax.random.randint(jax.random.fold_in(_rk, 8), (2,), 0, max(1, 1024 // 4) + 1, jnp.int32)
        _ctx_768P = jax.random.normal(jax.random.fold_in(_rk, 11), (2, 16, 192), jnp.float32)
        _ctx_768c = jax.random.dirichlet(jax.random.fold_in(_rk, 511), 0.3 * jnp.ones((16,), jnp.float32), (2, 1024))
        _ctx_768t = jnp.einsum('bsk,bkd->bsd', _ctx_768c, _ctx_768P)
        _ctx_768t = _ctx_768t * jax.lax.rsqrt(jnp.mean(jnp.square(_ctx_768t)) + 1e-12) * 0.953939
        ctx_768 = 2.09791e-05 + 1.00001 * (_ctx_768t + 0.3 * jax.random.normal(jax.random.fold_in(_rk, 611), (2, 1024, 192), jnp.float32))
        _validS = jnp.arange(512)[None, :] < _lenS[:, None]
        _validS2 = jnp.arange(1024)[None, :] < _lenS2[:, None]
        _causal = jnp.tril(jnp.ones((512, 512), dtype=bool))
        mask_BxS_bk0 = jnp.logical_not(jnp.broadcast_to(_validS[:, :], (2, 512)))
        return (x, ctx_768, mask_BxS_bk0)
    x, ctx_768, mask_BxS_bk0 = _rec_inputs()

    def _L0_attn_setup():
        import jax, jax.numpy as jnp
        import numpy as np
        D_MODEL = 256
        N_HEADS = 16
        HEAD_DIM = D_MODEL // N_HEADS
        BATCH = 2
        SEQ = 512

        def _alibi_bias(seq_len, n_heads, dtype):
            slopes = 1.0 / 2.0 ** (jnp.arange(n_heads, dtype=dtype) / n_heads)
            rel = jnp.arange(seq_len, dtype=dtype)[None, :] - jnp.arange(seq_len, dtype=dtype)[:, None]
            return slopes[:, None, None] * rel[None, :, :]
        key = jax.random.key(seed)
        ks = jax.random.split(key, 9)
        s = 0.02
        return {'x': jax.random.normal(ks[0], (BATCH, SEQ, D_MODEL), dtype=jnp.float32), 'Wq': jax.random.normal(ks[1], (D_MODEL, D_MODEL), dtype=jnp.float32) * s, 'bq': jnp.zeros((D_MODEL,), dtype=jnp.float32), 'Wk': jax.random.normal(ks[2], (D_MODEL, D_MODEL), dtype=jnp.float32) * s, 'bk': jnp.zeros((D_MODEL,), dtype=jnp.float32), 'Wv': jax.random.normal(ks[3], (D_MODEL, D_MODEL), dtype=jnp.float32) * s, 'bv': jnp.zeros((D_MODEL,), dtype=jnp.float32), 'Wo': jax.random.normal(ks[4], (D_MODEL, D_MODEL), dtype=jnp.float32) * s, 'bo': jnpp_zeros() if False else jnp.zeros((D_MODEL,), dtype=jnp.float32)}
    _L0_attn_all = _L0_attn_setup()
    _L0_attn_in = {k: v for k, v in _L0_attn_all.items() if k in ('Wq', 'bq', 'Wk', 'bk', 'Wv', 'bv', 'Wo', 'bo')}
    del _L0_attn_all

    def _L0_xattn_setup():
        import jax, jax.numpy as jnp
        import numpy as np
        NUM_HEADS = 16
        key = jax.random.key(seed)
        k1, k2, k3, k4, k5 = jax.random.split(key, 5)
        B, N, C = (4, 512, 256)
        N2, Cy = (256, 192)
        x = jax.random.normal(k1, (B, N, C), dtype=jnp.float32)
        y = jax.random.normal(k2, (B, N2, Cy), dtype=jnp.float32)
        pad_mask = jax.random.randint(k3, (B, N), 0, 2).astype(jnp.bool_)
        Wq = jax.random.normal(k4, (C, C), dtype=jnp.float32) * C ** (-0.5)
        Wkv = jax.random.normal(k5, (2 * C, Cy), dtype=jnp.float32) * Cy ** (-0.5)
        return {'x': x, 'y': y, 'pad_mask': pad_mask, 'Wq': Wq, 'Wkv': Wkv}
    _L0_xattn_all = _L0_xattn_setup()
    _L0_xattn_in = {k: v for k, v in _L0_xattn_all.items() if k in ('Wq', 'Wkv')}
    del _L0_xattn_all

    def _L0_ffn_setup():
        import jax, jax.numpy as jnp
        import numpy as np
        DIM = 256

        def _reference_tuple_inner(x, W_r, W_k, W_v, mu_r, mu_k):
            B, T, C = x.shape
            x_prev = jnp.concatenate([jnp.zeros((B, 1, C), x.dtype), x[:, :-1, :]], axis=1)
            xr = mu_r * x + (1.0 - mu_r) * x_prev
            xk = mu_k * x + (1.0 - mu_k) * x_prev
            r = jax.nn.sigmoid(jnp.einsum('btc,dc->btd', xr, W_r))
            k = jnp.einsum('btc,dc->btd', xk, W_k)
            k_act = jnp.square(jax.nn.relu(k))
            out = r * jnp.einsum('btc,dc->btd', k_act, W_v)
            new_state = x[:, -1, :]
            return (out, new_state)
        key = jax.random.key(seed)
        ks = jax.random.split(key, 6)
        B, T, C = (8, 512, DIM)
        x = jax.random.normal(ks[0], (B, T, C), dtype=jnp.float32)
        s = 1.0 / np.sqrt(C)
        W_r = jax.random.uniform(ks[1], (C, C), jnp.float32, -s, s)
        W_k = jax.random.uniform(ks[2], (C, C), jnp.float32, -s, s)
        W_v = jax.random.uniform(ks[3], (C, C), jnp.float32, -s, s)
        mu_r = jax.random.uniform(ks[4], (C,), jnp.float32)
        mu_k = jax.random.uniform(ks[5], (C,), jnp.float32)
        return {'x': x, 'W_r': W_r, 'W_k': W_k, 'W_v': W_v, 'mu_r': mu_r, 'mu_k': mu_k}
    _L0_ffn_all = _L0_ffn_setup()
    _L0_ffn_in = {k: v for k, v in _L0_ffn_all.items() if k in ('W_r', 'W_k', 'W_v', 'mu_r', 'mu_k')}
    del _L0_ffn_all
    return {'x': x, 'ctx_768': ctx_768, 'mask_BxS_bk0': mask_BxS_bk0, 'L0_attn_Wq': _L0_attn_in['Wq'], 'L0_attn_bq': _L0_attn_in['bq'], 'L0_attn_Wk': _L0_attn_in['Wk'], 'L0_attn_bk': _L0_attn_in['bk'], 'L0_attn_Wv': _L0_attn_in['Wv'], 'L0_attn_bv': _L0_attn_in['bv'], 'L0_attn_Wo': _L0_attn_in['Wo'], 'L0_attn_bo': _L0_attn_in['bo'], 'L0_xattn_Wq': _L0_xattn_in['Wq'], 'L0_xattn_Wkv': _L0_xattn_in['Wkv'], 'L0_ffn_W_r': _L0_ffn_in['W_r'], 'L0_ffn_W_k': _L0_ffn_in['W_k'], 'L0_ffn_W_v': _L0_ffn_in['W_v'], 'L0_ffn_mu_r': _L0_ffn_in['mu_r'], 'L0_ffn_mu_k': _L0_ffn_in['mu_k']}

def reference(x, ctx_768, mask_BxS_bk0, L0_attn_Wq, L0_attn_bq, L0_attn_Wk, L0_attn_bk, L0_attn_Wv, L0_attn_bv, L0_attn_Wo, L0_attn_bo, L0_xattn_Wq, L0_xattn_Wkv, L0_ffn_W_r, L0_ffn_W_k, L0_ffn_W_v, L0_ffn_mu_r, L0_ffn_mu_k):
    import jax
    import jax.numpy as jnp

    def _L0_attn_ref(x, Wq, bq, Wk, bk, Wv, bv, Wo, bo):
        import jax, jax.numpy as jnp
        import numpy as np
        D_MODEL = 256
        N_HEADS = 16
        HEAD_DIM = D_MODEL // N_HEADS
        BATCH = 2
        SEQ = 512

        def _alibi_bias(seq_len, n_heads, dtype):
            slopes = 1.0 / 2.0 ** (jnp.arange(n_heads, dtype=dtype) / n_heads)
            rel = jnp.arange(seq_len, dtype=dtype)[None, :] - jnp.arange(seq_len, dtype=dtype)[:, None]
            return slopes[:, None, None] * rel[None, :, :]
        B, S, D = x.shape
        H, Hd = (N_HEADS, HEAD_DIM)
        scale = Hd ** (-0.5)
        Q = (x @ Wq + bq).reshape(B, S, H, Hd)
        K = (x @ Wk + bk).reshape(B, S, H, Hd)
        V = (x @ Wv + bv).reshape(B, S, H, Hd)
        scores = jnp.einsum('bqhd,bkhd->bhqk', Q, K) * scale
        scores = scores + _alibi_bias(S, H, x.dtype)[None]
        attn = jax.nn.softmax(scores, axis=-1)
        out = jnp.einsum('bhqk,bkhd->bqhd', attn, V).reshape(B, S, D)
        return out @ Wo + bo

    def _L0_xattn_ref(x, y, pad_mask, Wq, Wkv):
        import jax, jax.numpy as jnp
        import numpy as np
        NUM_HEADS = 16
        B, N, C = x.shape
        N2 = y.shape[1]
        H = NUM_HEADS
        d = C // H
        scale = d ** (-0.5)
        q = (x @ Wq.T).reshape(B, N, H, d).transpose(0, 2, 1, 3)
        kv = (y @ Wkv.T).reshape(B, N2, 2, H, d).transpose(2, 0, 3, 1, 4)
        k, v = (kv[0], kv[1])
        attn = jnp.einsum('bhnd,bhmd->bhnm', q * scale, k)
        attn = jnp.where(pad_mask[:, None, :, None], attn, jnp.float32(-1000000000.0))
        attn = jax.nn.softmax(attn, axis=-1)
        out = jnp.einsum('bhnm,bhmd->bhnd', attn, v)
        return out.transpose(0, 2, 1, 3).reshape(B, N, C)

    def _L0_ffn_ref(x, W_r, W_k, W_v, mu_r, mu_k):
        import jax, jax.numpy as jnp
        import numpy as np
        DIM = 256

        def _reference_tuple_inner(x, W_r, W_k, W_v, mu_r, mu_k):
            B, T, C = x.shape
            x_prev = jnp.concatenate([jnp.zeros((B, 1, C), x.dtype), x[:, :-1, :]], axis=1)
            xr = mu_r * x + (1.0 - mu_r) * x_prev
            xk = mu_k * x + (1.0 - mu_k) * x_prev
            r = jax.nn.sigmoid(jnp.einsum('btc,dc->btd', xr, W_r))
            k = jnp.einsum('btc,dc->btd', xk, W_k)
            k_act = jnp.square(jax.nn.relu(k))
            out = r * jnp.einsum('btc,dc->btd', k_act, W_v)
            new_state = x[:, -1, :]
            return (out, new_state)
        return _reference_tuple_inner(x, W_r, W_k, W_v, mu_r, mu_k)[0]
    x = _layernorm(x + _L0_attn_ref(x, L0_attn_Wq, L0_attn_bq, L0_attn_Wk, L0_attn_bk, L0_attn_Wv, L0_attn_bv, L0_attn_Wo, L0_attn_bo), axis=-1)
    x = _layernorm(x + _L0_xattn_ref(x, ctx_768, mask_BxS_bk0, L0_xattn_Wq, L0_xattn_Wkv), axis=-1)
    x = _layernorm(x + _L0_ffn_ref(x, L0_ffn_W_r, L0_ffn_W_k, L0_ffn_W_v, L0_ffn_mu_r, L0_ffn_mu_k), axis=-1)
    return x

_drawn_inputs = setup_inputs


def setup_inputs(seed=0):
    import zlib

    import numpy as np

    out = dict(_drawn_inputs(seed))
    spreads = {'L0_attn_bq': (0.0, 0.8),
     'L0_attn_bk': (0.0, 0.8),
     'L0_attn_bv': (0.0, 0.278),
     'L0_attn_bo': (0.0, 0.1)}
    factors = {'L0_attn_Wq': 8.0, 'L0_attn_Wk': 8.0, 'L0_ffn_W_r': 2.726, 'L0_ffn_mu_r': 6.645}
    for name, (base, spread) in spreads.items():
        noise = np.random.default_rng([zlib.crc32(name.encode()), seed]).standard_normal(out[name].shape)
        drawn = base * np.exp(spread * noise) if base else spread * noise
        out[name] = jnp.asarray(drawn.astype(out[name].dtype))
    for name, factor in factors.items():
        out[name] = (out[name] * factor).astype(out[name].dtype)
    return out
```

```python
from contextlib import ExitStack

import concourse.bass as bass
from concourse import mybir

F32 = mybir.dt.float32
BF16 = mybir.dt.bfloat16
I32 = mybir.dt.int32
U8 = mybir.dt.uint8
ALU = mybir.AluOpType
ACT = mybir.ActivationFunctionType
AX = mybir.AxisListType.X

P = 128
B, S, D = 2, 512, 256
H, HD = 16, 16
S2, DC = 1024, 192
CC = D // P
XC = 96
QT = S // P
KB = S // P
XKB = S2 // P
HG = 4
UNITS = H // HG
PAIRS = H // 2
VW = HD + 1
EPS = 1e-5
QSCALE = float(HD) ** -0.5
Q_PARTS = (0, 0, 0, 1, 1, 2)
K_PARTS = (0, 1, 2, 0, 1, 0)
SPLIT_ROWS = HD * len(Q_PARTS)
MAX_ROW = SPLIT_ROWS
SELF_ROWS = SPLIT_ROWS + 2 + 3
CROSS_ROWS = SPLIT_ROWS + 2
PRING = 6


def plan():
    order = []
    for dc in range(CC):
        order += [("proj", "q", 0, dc, 0), ("proj", "k", 0, dc, 0)]
    order += [("val", 0, 0), ("val", 0, 1)]
    side = [("proj", w, 1, dc, 0) for dc in range(CC) for w in "qk"]
    for b in range(B):
        side += [("ctxsum", b)]
        side += [("proj", "x", b, dc, half) for dc in range(CC) for half in range(2)]
        side += [("xval", b, i) for i in range(XKB // 2)] + [("mean", b)]
        if b == 0:
            side += [("val", 1, 0), ("val", 1, 1)]

    def post_self(b):
        return ([("attnT", b, dc) for dc in range(CC)] + [("wo", b, half) for half in range(2)] + [("ln1", b)]
                + [("x1T", b, dc) for dc in range(CC)] + [("proj", "c", b, dc, 0) for dc in range(CC)])

    late = post_self(0)
    for s in range(B * PAIRS + 3):
        for i in range(8):
            if s < B * PAIRS:
                order.append(("A", s, i))
            if 2 <= s < B * PAIRS + 2:
                order.append(("B", s - 2, i))
            if i == 3 and 1 <= s <= B * PAIRS:
                order.append(("M", s - 1))
            if s >= 4 and s % 2 == 0 and 2 <= i < 2 + KB:
                order.append(("C", (s - 4) // 2, i - 2))
                if i == 1 + KB:
                    order.append(("O", (s - 4) // 2))
            if i in ((1, 5) if s >= 2 else (0, 2, 4, 6)):
                queue = late if s > 2 * UNITS + 2 and late else side
                if queue:
                    order.append(queue.pop(0))
            if i == 7 and s >= 4 and s % 2 == 0:
                order.append(("norm", (s - 4) // 2))
        if s == PAIRS + 2:
            order.append(("kxread", 0))
        if s == B * PAIRS + 1:
            order.append(("kxread", 1))
    order += side + late + post_self(1)
    return order


def decoder_layer(nc, x, xT, ctxT, mask, wq, bq, wk, bk, wv, bv, wo, bo, xwqT, xwkvT, wrT, wkT, wvT, mur, muk,
                  k_rows, q_rows, ident, out):
    order = plan()
    items = [e for e in order if e[0] in ("proj", "val", "xval", "mean", "norm", "attnT", "wo", "x1T")]
    nth = {e: n for n, e in enumerate(items)}
    ON_ACT = ("xval", "mean", "attnT", "x1T")
    rank = {}
    for e in items:
        rank[e] = sum(1 for f in items[:nth[e] + 1] if (f[0] in ON_ACT) == (e[0] in ON_ACT))
    splits = [e for e in items if e[0] == "proj"]
    split_no = {e: k for k, e in enumerate(splits)}

    def fast(e):
        return e[1] == "c" or (e[1] in "qk" and e[2] == 0)

    split_rank = {e: sum(1 for f in splits[:split_no[e] + 1] if fast(f) == fast(e)) for e in splits}

    ctx = ExitStack()
    with ctx:
        def sb(name, shape, dt=F32):
            return ctx.enter_context(nc.sbuf_tensor(name, shape, dt))

        def ps(name, shape, dt=F32):
            return ctx.enter_context(nc.psum_tensor(name, shape, dt))

        def sem(name):
            return ctx.enter_context(nc.semaphore(name))

        ops = [sb(f"ops{b}", [P, 2, H, S], BF16) for b in range(B)]
        kx = [ops[b][:, :, :, :].rearrange("p a h t -> p (a h t)").rearrange("p (h t) -> p h t", h=H) for b in range(B)]
        probs = sb("probs", [P, PRING * KB * S])
        pself = probs[:, :].rearrange("p (r k t) -> p r k t", r=PRING, k=KB)
        pcross = probs[:, 0:2 * HG * XKB * P].rearrange("p (u j k t) -> p u j k t", u=2, j=HG, k=XKB)
        v_self = sb("v_self", [P, B, KB, H, VW])
        v_cross = sb("v_cross", [P, B, XKB, H, VW])
        x_sb = sb("x_sb", [P, B, QT, D])
        xT_sb = sb("xT_sb", [P, B, CC, S])
        ctx_sb = sb("ctx_sb", [P, 2, S2])
        qx = ctx_sb[:, :, :].rearrange("p a t -> p (a t)").bitcast(BF16).rearrange("p (b h t) -> p b h t", b=B, h=H)
        attn = sb("attn", [P, B, QT, D])
        w_q, w_k, w_v, w_o, w_xq = (sb(f"w{n}", [P, CC, D]) for n in ("q", "k", "v", "o", "xq"))
        w_kv = sb("w_kv", [XC, 2, 2 * D])
        q32 = sb("q32", [P, 2, S])
        parts = sb("parts", [P, 2, 3, S], BF16)
        outT = sb("outT", [P, S])
        identf = sb("identf", [P, P])
        identb = sb("identb", [P, P], BF16)
        bq_c, bk_c = sb("bq_c", [P, CC]), sb("bk_c", [P, CC])
        bv_r, bo_r = sb("bv_r", [P, D]), sb("bo_r", [P, D])
        mur_c, muk_c = sb("mur_c", [P, CC]), sb("muk_c", [P, CC])
        om_r, om_k = sb("om_r", [P, CC]), sb("om_k", [P, CC])
        meanv = sb("meanv", [P, B, D])
        csum = sb("csum", [XC, 2])
        csum_r = sb("csum_r", [XC, 2, P])
        mx = sb("mx", [P, 2, 2, QT])
        mres = sb("mres", [P, 2, 2, QT])
        mparts = sb("mparts", [P, 2, 2, QT, 2], BF16)
        rden = sb("rden", [P, QT, HG])
        stats = sb("stats", [P, QT, 6])
        mv = sb("mv", [P, QT, 2])
        ve = sb("ve", [P, QT])
        rstd = sb("rstd", [P, QT])
        nhalf = sb("nhalf", [P, QT])
        minus = sb("minus", [P, HG])
        mask_q = sb("mask_q", [P, B, QT], U8)
        mask_row = sb("mask_row", [1, B, QT, P], U8)
        live = sb("live", [1, B, QT])
        weight = sb("weight", [1, B, QT])
        behind = sb("behind", [1, B])
        count_i = sb("count_i", [1, B], I32)
        xm = sb("xm", [P, HG, 2])
        xmax = sb("xmax", [P, HG])
        xres = sb("xres", [P, HG])
        xparts = sb("xparts", [P, HG, 2], BF16)
        xrd = sb("xrd", [P, HG])
        tile_att = sb("tile_att", [P, D])
        tile_sel = sb("tile_sel", [P, D])
        mcur = sb("mcur", [P, 1], U8)
        gate_pad = sb("gate_pad", [P, 1])
        cursor = [0]

        def in_probs(*shape):
            n = 1
            for d in shape:
                n *= d
            a = probs[:, cursor[0]:cursor[0] + n]
            cursor[0] += n
            assert cursor[0] <= PRING * KB * S
            return a
        w_r, w_k2, w_v2 = (in_probs(CC, D).rearrange("p (c d) -> p c d", c=CC) for _ in range(3))
        x2T = in_probs(B, CC, S + 1).rearrange("p (b c t) -> p b c t", b=B, c=CC)
        xr = in_probs(B, CC, S).rearrange("p (b c t) -> p b c t", b=B, c=CC)
        xk = in_probs(B, CC, S).rearrange("p (b c t) -> p b c t", b=B, c=CC)
        kact = in_probs(CC, S).rearrange("p (c t) -> p c t", c=CC)
        sig = in_probs(QT, D).rearrange("p (c t) -> p c t", c=QT)

        psA = ps("psA", [P, 2, S])
        psB = ps("psB", [P, 2, S])
        psC = ps("psC", [P, S])
        psT = ps("psT", [P, 2, S], BF16)
        psN = ps("psN", [P, 2, S])

        scr = {w: nc.dram_tensor(f"scr_{w}", [B, CC, 3, HD, H // CC, S2 if w == "x" else S], BF16).ap() for w in "qkxc"}

        in_qk, in_ident, in_const, in_v, in_ctx, in_late, in_mask, in_ffn = (
            sem(n) for n in ("in_qk", "in_ident", "in_const", "in_v", "in_ctx", "in_late", "in_mask", "in_ffn"))
        init_done = sem("init_done")
        bank_full = sem("bank_full")
        dve_emptied, act_emptied = sem("dve_emptied"), sem("act_emptied")
        dve_split, pool_split = sem("dve_split"), sem("pool_split")
        scr_written = [sem(f"scr_written{n}") for n in range(2)]
        rows_in = [[sem(f"rows_in{b}{dc}") for dc in range(CC)] for b in range(B)]
        kx_in = [sem(f"kx_in{b}") for b in range(B)]
        qx_in = [sem(f"qx_in{b}") for b in range(B)]
        csum_ready = sem("csum_ready")
        a_full, a_max = sem("a_full"), sem("a_max")
        max_parts, max_turned, max_rows = sem("max_parts"), sem("max_turned"), sem("max_rows")
        b_full, exp_done = sem("b_full"), sem("exp_done")
        c_done, outT_ready = sem("c_done"), sem("outT_ready")
        var_ready, rstd_ready, ln_done = sem("var_ready"), sem("rstd_ready"), sem("ln_done")
        residual = sem("residual")
        dve_step, pool_step, act_step = sem("dve_step"), sem("pool_step"), sem("act_step")
        count_ready = sem("count_ready")
        passed = sem("passed")
        gate = [sem(f"gate{b}") for b in range(B)]
        X = [{n: sem(f"x{n}{b}") for n in ("a_full", "a_max", "max2", "parts", "turned", "rows", "b_full", "exp", "c_done",
                                           "outT", "n_full", "n_done")} for b in range(B)]
        XTOT = {"a_full": 32, "a_max": 32, "parts": 12, "max2": 4, "turned": 4, "rows": 4, "b_full": 32, "exp": 32, "c_done": 4,
                "outT": 4, "n_full": 4, "n_done": 11, "qx": 16 * 12}
        cross_done = sem("cross_done")
        f_full, f_act, f_dve = sem("f_full"), sem("f_act"), sem("f_dve")
        mix_done, sq_done, out_ready, stored = sem("mix_done"), sem("sq_done"), sem("out_ready"), sem("stored")

        def bank(e):
            return psN[:, nth[e] % 2, :]

        def wait_emptied(eng, e):
            eng.wait_ge(act_emptied if e[0] in ON_ACT else dve_emptied, rank[e])

        def wait_split(eng, e):
            eng.wait_ge(dve_split if fast(e) else pool_split, split_rank[e])

        def wait_written(eng, k):
            eng.wait_ge(scr_written[k % 2], 16 * (k // 2 + 1))

        job = []
        for s in range(UNITS + 2):
            for i in range(8):
                if s < UNITS:
                    job.append(("A", s, i))
                if i < 4 and s >= 2:
                    job += [("C", s - 2, 2 * i), ("C", s - 2, 2 * i + 1)]
                if i == 3:
                    if s >= 2:
                        job += [("O", s - 2), ("norm", s - 2)]
                    if 1 <= s <= UNITS:
                        job.append(("M", s - 1))
                if i >= 4 and 1 <= s <= UNITS:
                    job.append(("B", s - 1, i - 4))
            if 1 <= s <= UNITS:
                job += [("B", s - 1, i) for i in range(4, 8)]

        def tiles(eng, b):
            eng.wait_ge(count_ready, 1)
            count = eng.value_load(count_i[0:1, b:b + 1], min_val=1, max_val=QT)
            with eng.Fori(0, count) as n:
                def at(name, c):
                    return n * XTOT[name] + c
                eng.wait_ge(gate[b], n + 1)
                eng.sem_inc(passed, 1)
                yield (QT - 1) - n, at

        block = ctx.enter_context(nc.Block())

        @block.sync
        def _(sp):
            def load(dst, src, s):
                sp.dma_start(dst, src).then_inc(s, 16)

            def wide(w):
                return w.rearrange("(c p) n -> p c n", p=P)
            load(xT_sb[:, 0, :, :], xT[0].rearrange("(c p) t -> p c t", p=P), in_qk)
            load(w_q[:, :, :], wide(wq), in_qk)
            load(w_k[:, :, :], wide(wk), in_qk)
            load(bq_c[:, :], bq, in_qk)
            load(bk_c[:, :], bk, in_qk)
            load(w_v[:, :, :], wide(wv), in_v)
            load(bv_r[:, :], bv.rearrange("(a n) -> a n", a=1).broadcast_to([P, D]), in_v)
            load(xT_sb[:, 1, :, :], xT[1].rearrange("(c p) t -> p c t", p=P), in_v)
            load(ctx_sb[0:XC, :, :], ctxT[0].rearrange("(c p) t -> p c t", p=XC), in_ctx)
            load(w_kv[:, :, :], xwkvT.rearrange("(c p) n -> p c n", p=XC), in_ctx)
            for e in order:
                if e[0] == "proj":
                    _, w, b, dc, half = e
                    k = split_no[e]
                    cols = slice(half * S, half * S + S)
                    wait_split(sp, e)
                    sp.dma_start(scr[w][b, dc].rearrange("j d h t -> (d h) j t")[:, :, cols],
                                 parts[:, k % 2, :, :]).then_inc(scr_written[k % 2], 16)
                    if w in "qk":
                        wait_written(sp, k)
                        for g, j in enumerate(Q_PARTS if w == "q" else K_PARTS):
                            load(ops[b][HD * g:HD * g + HD, 0 if w == "q" else 1, 8 * dc:8 * dc + 8, :],
                                 scr[w][b, dc, j], rows_in[b][dc])
                elif e == ("ctxsum", 1):
                    sp.wait_ge(bank_full, nth[("mean", 0)] + 1)
                    sp.wait_ge(csum_ready, 1)
                    load(ctx_sb[0:XC, :, :], ctxT[1].rearrange("(c p) t -> p c t", p=XC), in_ctx)
                elif e[0] == "kxread":
                    b = e[1]
                    last = ("proj", "x", b, CC - 1, 1)
                    wait_written(sp, split_no[last]) 
                    wait_written(sp, split_no[last] - 1)
                    sp.wait_ge(b_full, 8 * PAIRS * (b + 1))
                    for dc in range(CC):
                        for g, j in enumerate(K_PARTS):
                            load(kx[b][HD * g:HD * g + HD, 8 * dc:8 * dc + 8, :], scr["x"][b, dc, j], kx_in[b])
                    load(kx[b][MAX_ROW:MAX_ROW + 2, 0:H // 2, :], k_rows[0:2, :, :].rearrange("r h t -> r (h t)")
                         .rearrange("r (h t) -> r h t", t=S2), kx_in[b])
            for b in range(B):
                last = ("proj", "c", b, CC - 1, 0)
                wait_written(sp, split_no[last]) 
                wait_written(sp, split_no[last] - 1)
                for t, at in tiles(sp, b):
                    for dc in range(CC):
                        for g, j in enumerate(Q_PARTS):
                            load(qx[HD * g:HD * g + HD, b, 8 * dc:8 * dc + 8, :],
                                 scr["c"][b, dc, j][:, :, bass.ts(t, P)], qx_in[b])
            sp.wait_ge(cross_done, 1)
            for dst, src in ((w_r, wrT), (w_k2, wkT), (w_v2, wvT)):
                load(dst, wide(src), in_ffn)
            for b in range(B):
                sp.wait_ge(out_ready, b + 1)
                load(out[b].rearrange("(q p) d -> p q d", p=P), x_sb[:, b, :, :], stored)
            sp.wait_ge(stored, 16 * B)

        @block.gpsimd
        def _(pool):
            steps = [0]

            def step(ins):
                steps[0] += 1
                ins.then_inc(pool_step, 1)
                pool.wait_ge(pool_step, steps[0])

            pool.memset(v_self[:, :, :, :, HD:VW], 1.0).then_inc(init_done, 1)
            pool.memset(v_cross[:, :, :, :, HD:VW], 1.0).then_inc(init_done, 1)
            pool.memset(minus[:, :], -1.0).then_inc(init_done, 1)
            pool.memset(nhalf[:, :], -0.5).then_inc(init_done, 1)

            pool.wait_ge(init_done, 6)
            pool.wait_ge(in_late, 16 * 7)
            for b in range(B):
                for q in range(QT):
                    ins = pool.tensor_tensor(x_sb[:, b, q, :], x_sb[:, b, q, :], bo_r[:, :], ALU.add)
                ins.then_inc(residual, 1)
            for e in order:
                if e[0] == "proj" and not fast(e):
                    k = split_no[e]
                    pool.wait_ge(dve_emptied, rank[e])
                    if k >= 2:
                        wait_written(pool, k - 2)
                    v, pt = q32[:, k % 2, :], parts[:, k % 2, :, :]
                    step(pool.tensor_copy(pt[:, 0, :], v))
                    step(pool.tensor_tensor(v, v, pt[:, 0, :], ALU.subtract))
                    step(pool.tensor_copy(pt[:, 1, :], v))
                    pool.tensor_tensor(pt[:, 2, :], v, pt[:, 1, :], ALU.subtract).then_inc(pool_split, 1)
                elif e[0] == "M":
                    p = e[1]
                    m, r, o = mx[:, p % 2, :, :], mres[:, p % 2, :, :], mparts[:, p % 2, :, :, :]
                    pool.wait_ge(a_max, 8 * (p + 1))
                    if p >= 2:
                        pool.wait_ge(max_turned, p - 1)
                    step(pool.tensor_scalar(o[:, :, :, 0], m, -1.0, None, ALU.mult))
                    step(pool.tensor_tensor(r, m, o[:, :, :, 0], ALU.add))
                    pool.tensor_scalar(o[:, :, :, 1], r, -1.0, None, ALU.mult).then_inc(max_parts, 1)
                elif e[0] == "ln1":
                    pool.wait_ge(var_ready, e[1] + 1)
                    pool.tensor_tensor(rstd[:, :], ve[:, :], nhalf[:, :], ALU.pow).then_inc(rstd_ready, 1)
            for b in range(B):
                for t, at in tiles(pool, b):
                    for e in job:
                        if e[0] == "M":
                            g = e[1]
                            pool.wait_ge(X[b]["max2"], at("max2", g + 1))
                            if g >= 1:
                                pool.wait_ge(X[b]["turned"], at("turned", g))
                            pool.tensor_tensor(xparts[:, :, 0], xmax[:, :], minus[:, :], ALU.mult)\
                                .then_inc(X[b]["parts"], 1)
                            pool.wait_ge(X[b]["parts"], at("parts", 3 * g + 1))
                            pool.tensor_tensor(xres[:, :], xmax[:, :], xparts[:, :, 0], ALU.add)\
                                .then_inc(X[b]["parts"], 1)
                            pool.wait_ge(X[b]["parts"], at("parts", 3 * g + 2))
                            pool.tensor_tensor(xparts[:, :, 1], xres[:, :], minus[:, :], ALU.mult)\
                                .then_inc(X[b]["parts"], 1)
            for n in range(2 * B):
                pool.wait_ge(var_ready, B + n + 1)
                pool.tensor_tensor(rstd[:, :], ve[:, :], nhalf[:, :], ALU.pow).then_inc(rstd_ready, 1)

        @block.scalar
        def _(act):
            act.dma_start(identf[:, :], ident).then_inc(in_ident, 16)
            for b in range(B):
                act.dma_start(ops[b][MAX_ROW:SELF_ROWS, 0, :, :], q_rows).then_inc(in_const, 16)
                act.dma_start(ops[b][MAX_ROW:SELF_ROWS, 1, :, :], k_rows).then_inc(in_const, 16)
            act.dma_start(mask_row[0:1, :, :, :], mask.rearrange("(a b) (q p) -> a b q p", a=1, p=P))\
               .then_inc(in_mask, 16)
            with nc.allow_non_contiguous_dma(reason="one byte for each query"):
                act.dma_start(mask_q[:, :, :], mask.rearrange("b (q p) -> p b q", p=P)).then_inc(in_mask, 16)
            act.dma_start(x_sb[:, 0, :, :], x[0].rearrange("(q p) d -> p q d", p=P)).then_inc(in_late, 16)
            act.dma_start(x_sb[:, 1, :, :], x[1].rearrange("(q p) d -> p q d", p=P)).then_inc(in_late, 16)
            act.dma_start(bo_r[:, :], bo.rearrange("(a n) -> a n", a=1).broadcast_to([P, D])).then_inc(in_late, 16)
            act.dma_start(w_o[:, :, :], wo.rearrange("(c p) n -> p c n", p=P)).then_inc(in_late, 16)
            act.dma_start(w_xq[:, :, :], xwqT.rearrange("(c p) n -> p c n", p=P)).then_inc(in_late, 16)
            act.dma_start(mur_c[:, :], mur).then_inc(in_late, 16)
            act.dma_start(muk_c[:, :], muk).then_inc(in_late, 16)
            act.wait_ge(in_ident, 16)
            act.activation(identb[:, :], identf[:, :], ACT.Copy).then_inc(init_done, 1)
            for e in order:
                kind = e[0]
                if kind == "B":
                    _, p, i = e
                    n, head = 8 * p + i, 2 * p + i // 4
                    if i % 4 == 0 and head >= PRING:
                        act.wait_ge(c_done, (head - PRING) // HG + 1)
                    act.wait_ge(b_full, n + 1)
                    act.activation(pself[:, head % PRING, i % 4, :], psB[:, n % 2, :], ACT.Exp).then_inc(exp_done, 1)
                elif kind == "M":
                    p = e[1]
                    b, h = p // PAIRS, 2 * (p % PAIRS)
                    act.wait_ge(max_turned, p + 1)
                    act.activation(ops[b][MAX_ROW:MAX_ROW + 2, 0, h:h + 2, :], psT[0:2, :, :], ACT.Copy)\
                       .then_inc(max_rows, 1)
                elif kind == "O":
                    u = e[1]
                    act.wait_ge(c_done, u + 1)
                    if u >= 1:
                        act.wait_ge(bank_full, nth[("norm", u - 1)] + 1)
                    act.activation(outT[:, :], psC[:, :], ACT.Copy).then_inc(outT_ready, 1)
                elif kind in ON_ACT:
                    act.wait_ge(bank_full, nth[e] + 1)
                    bk_ = bank(e)
                    if kind == "xval":
                        _, b, i = e
                        for j in range(2):
                            ins = act.activation(v_cross[:, b, 2 * i + j, :, 0:HD],
                                                 bk_[:, j * D:j * D + D].rearrange("p (h d) -> p h d", h=H), ACT.Copy)
                    elif kind == "mean":
                        ins = act.activation(meanv[:, e[1], :], bk_[:, 0:D], ACT.Copy)
                    else:
                        ins = act.activation(xT_sb[:, e[1], e[2], :], bk_, ACT.Copy)
                    ins.then_inc(act_emptied, 1)
            for b in range(B):
                for t, at in tiles(act, b):
                    for e in job:
                        if e[0] == "B":
                            _, g, i = e
                            act.wait_ge(X[b]["b_full"], at("b_full", 8 * g + i + 1))
                            if g >= 2 and i == 0:
                                act.wait_ge(X[b]["c_done"], at("c_done", g - 1))
                            act.activation(pcross[:, g % 2, i // 2, 4 * (i % 2):4 * (i % 2) + 4, :]
                                           .rearrange("p k t -> p (k t)"), psB[:, i % 2, :], ACT.Exp)\
                               .then_inc(X[b]["exp"], 1)
                        elif e[0] == "M":
                            g = e[1]
                            act.wait_ge(X[b]["turned"], at("turned", g + 1))
                            act.activation(qx[MAX_ROW:MAX_ROW + 2, b, HG * g:HG * g + HG, :],
                                           psT[0:2, 0, :].rearrange("p (h t) -> p h t", h=HG), ACT.Copy)\
                               .then_inc(X[b]["rows"], 1)
                        elif e[0] == "O":
                            g = e[1]
                            act.wait_ge(X[b]["c_done"], at("c_done", g + 1))
                            if g >= 1:
                                act.wait_ge(X[b]["n_full"], at("n_full", g))
                            act.activation(outT[:, 0:P], psC[:, 0:P], ACT.Copy).then_inc(X[b]["outT"], 1)
            for b in range(B):
                base = 8 * b
                for cc in range(CC):
                    act.wait_ge(f_full, base + cc + 1)
                    act.activation(x2T[:, b, cc, 1:S + 1], psN[:, cc % 2, :], ACT.Copy).then_inc(f_act, 1)
                for dc in range(CC):
                    act.wait_ge(f_full, base + 2 + dc + 1)
                    if b:
                        act.wait_ge(f_full, 8)
                    act.activation(kact[:, dc, :], psN[:, dc % 2, :], ACT.Relu).then_inc(act_step, 1)
                    act.wait_ge(act_step, 4 * b + 2 * dc + 1)
                    act.activation(kact[:, dc, :], kact[:, dc, :], ACT.Square).then_inc(act_step, 1)
                for half in range(2):
                    act.wait_ge(f_full, base + 4 + half + 1)
                    if b:
                        act.wait_ge(f_dve, 2)
                    act.activation(sig[:, 2 * half:2 * half + 2, :].rearrange("p q d -> p (q d)"),
                                   psN[:, half % 2, :], ACT.Sigmoid).then_inc(f_act, 1)

        @block.vector
        def _(dve):
            steps = [0]

            def step(ins):
                steps[0] += 1
                ins.then_inc(dve_step, 1)
                dve.wait_ge(dve_step, steps[0])

            lns = [0]

            def layer_norm(b):
                for q in range(QT):
                    ins = dve.bn_stats(stats[:, q, :], x_sb[:, b, q, :])
                step(ins)
                for q in range(QT):
                    ins = dve.bn_aggr(mv[:, q, :], stats[:, q, :])
                step(ins)
                dve.tensor_scalar(ve[:, :], mv[:, :, 1], EPS, None, ALU.add).then_inc(var_ready, 1)
                lns[0] += 1
                dve.wait_ge(rstd_ready, lns[0])
                for q in range(QT):
                    ins = dve.tensor_scalar(x_sb[:, b, q, :], x_sb[:, b, q, :], mv[:, q, 0:1], rstd[:, q:q + 1],
                                            ALU.subtract, ALU.mult)
                return ins

            dve.memset(psC[:, :], 0.0).then_inc(init_done, 1)
            for q in range(QT):
                ins = dve.memset(weight[0:1, :, q:q + 1], float(QT - 1 - q))
            dve.wait_ge(in_mask, 32)
            step(dve.tensor_reduce(live[0:1, :, :], mask_row[0:1, :, :, :], AX, ALU.max))
            step(dve.tensor_tensor(live[0:1, :, :], live[0:1, :, :], weight[0:1, :, :], ALU.mult))
            step(dve.tensor_reduce(behind[0:1, :], live[0:1, :, :], AX, ALU.max))
            dve.tensor_scalar(count_i[0:1, :], behind[0:1, :], 1.0, None, ALU.add).then_inc(count_ready, 1)
            for e in order:
                kind = e[0]
                if kind == "A":
                    _, p, i = e
                    if i == 0 and p >= 2:
                        dve.wait_ge(max_parts, p - 1)
                    dve.wait_ge(a_full, 8 * p + i + 1)
                    dve.tensor_reduce(mx[:, p % 2, i // 4, i % 4:i % 4 + 1], psA[:, i % 2, :], AX, ALU.max)\
                       .then_inc(a_max, 1)
                elif kind == "ctxsum":
                    b = e[1]
                    dve.wait_ge(in_ctx, 16 * (2 + b))
                    step(dve.tensor_reduce(csum[:, :], ctx_sb[0:XC, :, :], AX, ALU.add))
                    if b:
                        dve.wait_ge(bank_full, nth[("mean", 0)] + 1)
                    dve.tensor_scalar(csum_r[:, :, :], csum[:, :].unsqueeze(2).broadcast_to([XC, 2, P]), 1.0 / S2,
                                      None, ALU.mult).then_inc(csum_ready, 1)
                elif kind == "ln1":
                    b = e[1]
                    step(dve.memset(gate_pad[:, :], 0.0))
                    layer_norm(b).then_inc(ln_done, 1)
                elif kind in ("proj", "val", "norm", "wo"):
                    dve.wait_ge(bank_full, nth[e] + 1)
                    bk_ = bank(e)
                    if kind == "proj":
                        _, w, b, dc, half = e
                        k = split_no[e]
                        if k >= 2:
                            wait_split(dve, splits[k - 2])
                        v, pt = q32[:, k % 2, :], parts[:, k % 2, :, :]
                        if w == "q":
                            ins = dve.tensor_scalar(v, bk_, bq_c[:, dc:dc + 1], QSCALE, ALU.add, ALU.mult)
                        elif w == "k":
                            ins = dve.tensor_scalar(v, bk_, bk_c[:, dc:dc + 1], None, ALU.add)
                        else:
                            ins = dve.tensor_scalar(v, bk_, QSCALE if w == "c" else 1.0, None, ALU.mult)
                        ins.then_inc(dve_emptied, 1)
                        if fast(e):
                            dve.wait_ge(dve_emptied, rank[e])
                            if k >= 2:
                                wait_written(dve, k - 2)
                            step(dve.tensor_copy(pt[:, 0, :], v))
                            step(dve.tensor_tensor(v, v, pt[:, 0, :], ALU.subtract))
                            step(dve.tensor_copy(pt[:, 1, :], v))
                            dve.tensor_tensor(pt[:, 2, :], v, pt[:, 1, :], ALU.subtract).then_inc(dve_split, 1)
                    elif kind == "val":
                        _, b, half = e
                        dve.wait_ge(in_v, 16 * 3)
                        for j in range(2):
                            ins = dve.tensor_tensor(v_self[:, b, 2 * half + j, :, 0:HD],
                                                    bk_[:, j * D:j * D + D].rearrange("p (h d) -> p h d", h=H),
                                                    bv_r[:, :].rearrange("p (h d) -> p h d", h=H), ALU.add)
                        ins.then_inc(dve_emptied, 1)
                    elif kind == "norm":
                        u = e[1]
                        b, g = u // UNITS, u % UNITS
                        turned = bk_.rearrange("p (q j c) -> p q j c", q=QT, j=HG)
                        if u:
                            wait_emptied(dve, ("norm", u - 1))
                        step(dve.reciprocal(rden[:, :, :], turned[:, :, :, HD]))
                        for q in range(QT):
                            ins = dve.tensor_tensor(
                                attn[:, b, q, 64 * g:64 * g + 64].rearrange("p (j d) -> p j d", j=HG),
                                turned[:, q, :, 0:HD], rden[:, q, :].unsqueeze(2).broadcast_to([P, HG, HD]), ALU.mult)
                        ins.then_inc(dve_emptied, 1)
                    else:
                        _, b, half = e
                        dve.wait_ge(residual, b + 1)
                        r = x_sb[:, b, 2 * half:2 * half + 2, :].rearrange("p q d -> p (q d)")
                        dve.tensor_tensor(r, bk_, r, ALU.add).then_inc(dve_emptied, 1)
            for b in range(B):
                dve.wait_ge(bank_full, nth[("attnT", b, CC - 1)] + 1)
                wait_emptied(dve, ("mean", b))
                for q in range(QT):
                    ins = dve.tensor_copy(attn[:, b, q, :], meanv[:, b, :])
                step(ins)
                dve.memset(gate_pad[:, :], 0.0).then_inc(gate[b], 1)
                jobs = []
                for t, at in tiles(dve, b):
                    for e in job:
                        if e[0] == "A":
                            _, g, i = e
                            if i == 0 and g >= 1:
                                dve.wait_ge(X[b]["max2"], at("max2", g))
                            dve.wait_ge(X[b]["a_full"], at("a_full", 8 * g + i + 1))
                            dve.tensor_reduce(xm[:, i // 2, i % 2:i % 2 + 1], psA[:, i % 2, :], AX, ALU.max)\
                               .then_inc(X[b]["a_max"], 1)
                            if i == 7:
                                dve.wait_ge(X[b]["a_max"], at("a_max", 8 * (g + 1)))
                                if g >= 1:
                                    dve.wait_ge(X[b]["parts"], at("parts", 3 * g))
                                dve.tensor_reduce(xmax[:, :], xm[:, :, :], AX, ALU.max).then_inc(X[b]["max2"], 1)
                        elif e[0] == "norm":
                            g = e[1]
                            dve.wait_ge(X[b]["n_full"], at("n_full", g + 1))
                            turned = psN[:, g % 2, 0:P].rearrange("p (j c) -> p j c", j=HG)
                            if g:
                                dve.wait_ge(X[b]["n_done"], at("n_done", 2 * g))
                            dve.reciprocal(xrd[:, :], turned[:, :, HD]).then_inc(X[b]["n_done"], 1)
                            dve.wait_ge(X[b]["n_done"], at("n_done", 2 * g + 1))
                            dve.tensor_tensor(tile_att[:, 64 * g:64 * g + 64].rearrange("p (j d) -> p j d", j=HG),
                                              turned[:, :, 0:HD], xrd[:, :].unsqueeze(2).broadcast_to([P, HG, HD]),
                                              ALU.mult).then_inc(X[b]["n_done"], 1)
                    dve.wait_ge(X[b]["n_done"], at("n_done", 2 * UNITS))
                    dve.memset(gate_pad[:, :], 0.0)
                    dve.tensor_copy(mcur[:, :], mask_q[:, b, bass.ts(t, 1)]).then_inc(X[b]["n_done"], 1)
                    dve.tensor_copy(tile_sel[:, :], meanv[:, b, :]).then_inc(X[b]["n_done"], 1)
                    dve.wait_ge(X[b]["n_done"], at("n_done", 2 * UNITS + 2))
                    dve.memset(gate_pad[:, :], 0.0)
                    dve.copy_predicated(tile_sel[:, :], mcur[:, :].broadcast_to([P, D]), tile_att[:, :])\
                       .then_inc(X[b]["n_done"], 1)
                    dve.wait_ge(X[b]["n_done"], at("n_done", 2 * UNITS + 3))
                    dve.tensor_copy(attn[:, b, bass.ts(t, 1), :].rearrange("p a d -> p (a d)"), tile_sel[:, :])\
                       .then_inc(gate[b], 1)
            step(dve.memset(gate_pad[:, :], 0.0))
            for b in range(B):
                ins = dve.tensor_tensor(x_sb[:, b, :, :], x_sb[:, b, :, :], attn[:, b, :, :], ALU.add)
                step(ins)
                if b == 0:
                    dve.memset(x2T[:, :, :, 0:1], 0.0).then_inc(cross_done, 1)
                layer_norm(b).then_inc(ln_done, 1)
            step(dve.tensor_scalar(om_r[:, :], mur_c[:, :], -1.0, 1.0, ALU.mult, ALU.add))
            step(dve.tensor_scalar(om_k[:, :], muk_c[:, :], -1.0, 1.0, ALU.mult, ALU.add))
            for b in range(B):
                dve.wait_ge(f_act, 4 * b + 2)
                for mu, om, mixed in ((muk_c, om_k, xk), (mur_c, om_r, xr)):
                    for cc in range(CC):
                        ins = dve.tensor_scalar(mixed[:, b, cc, :], x2T[:, b, cc, 0:S], om[:, cc:cc + 1], None,
                                                ALU.mult)
                    step(ins)
                    for cc in range(CC):
                        ins = dve.scalar_tensor_tensor(out=mixed[:, b, cc, :], in0=x2T[:, b, cc, 1:S + 1],
                                                       scalar=mu[:, cc:cc + 1], in1=mixed[:, b, cc, :],
                                                       op0=ALU.mult, op1=ALU.add)
                    ins.then_inc(mix_done, 1)
                for half in range(2):
                    dve.wait_ge(f_full, 8 * b + 6 + half + 1)
                    dve.wait_ge(f_act, 4 * b + 2 + half + 1)
                    sl = sig[:, 2 * half:2 * half + 2, :].rearrange("p q d -> p (q d)")
                    dve.tensor_tensor(sl, psN[:, half % 2, :], sl, ALU.mult).then_inc(f_dve, 1)
                    dve.wait_ge(f_dve, 2 * b + half + 1)
                    r = x_sb[:, b, 2 * half:2 * half + 2, :].rearrange("p q d -> p (q d)")
                    ins = dve.tensor_tensor(r, r, sl, ALU.add)
                step(ins)
                layer_norm(b).then_inc(out_ready, 1)

        @block.tensor
        def _(pe):
            def project(e, terms):
                bk_ = bank(e)
                for c0, c1, pairs in terms:
                    for n, (l, r) in enumerate(pairs):
                        ins = pe.matmul(bk_[:, c0:c1], l, r, start=(n == 0), stop=(n == len(pairs) - 1))
                ins.then_inc(bank_full, 1)

            def turn(e, sources):
                bk_ = bank(e)
                for q, src in enumerate(sources):
                    ins = pe.transpose(bk_[:, q * P:q * P + P], src, identf[:, :])
                ins.then_inc(bank_full, 1)

            for e in order:
                kind = e[0]
                if e in nth and nth[e] >= 2:
                    wait_emptied(pe, items[nth[e] - 2])
                if kind == "proj":
                    _, w, b, dc, half = e
                    if w == "x":
                        pe.wait_ge(in_ctx, 16 * (2 + b))
                        project(e, [(0, S, [(w_kv[:, c, dc * P:dc * P + P], ctx_sb[0:XC, c, half * S:half * S + S])
                                            for c in range(2)])])
                    else:
                        if w == "c":
                            pe.wait_ge(in_late, 16 * 7)
                            wait_emptied(pe, ("x1T", b, CC - 1))
                        else:
                            pe.wait_ge(in_qk, 16 * 5)
                            if b:
                                pe.wait_ge(in_v, 16 * 3)
                        wt = {"q": w_q, "k": w_k, "c": w_xq}[w]
                        project(e, [(0, S, [(wt[:, c, dc * P:dc * P + P], xT_sb[:, b, c, :]) for c in range(CC)])])
                elif kind == "val":
                    _, b, half = e
                    pe.wait_ge(in_v, 16 * 3)
                    project(e, [(j * D, j * D + D, [(xT_sb[:, b, c, (2 * half + j) * P:(2 * half + j + 1) * P],
                                                     w_v[:, c, :]) for c in range(CC)]) for j in range(2)])
                elif kind == "xval":
                    _, b, i = e
                    pe.wait_ge(in_ctx, 16 * (2 + b))
                    project(e, [(j * D, j * D + D, [(ctx_sb[0:XC, c, (2 * i + j) * P:(2 * i + j + 1) * P],
                                                     w_kv[:, c, D:2 * D]) for c in range(2)]) for j in range(2)])
                elif kind == "mean":
                    pe.wait_ge(csum_ready, e[1] + 1)
                    project(e, [(0, D, [(csum_r[:, c, :], w_kv[:, c, D:2 * D]) for c in range(2)])])
                elif kind == "norm":
                    u = e[1]
                    pe.wait_ge(init_done, 6)
                    pe.wait_ge(outT_ready, u + 1)
                    turn(e, [outT[:, q * P:q * P + P] for q in range(QT)])
                elif kind == "attnT":
                    _, b, dc = e
                    wait_emptied(pe, ("norm", UNITS * b + UNITS - 1))
                    turn(e, [attn[:, b, q, dc * P:dc * P + P] for q in range(QT)])
                elif kind == "wo":
                    _, b, half = e
                    pe.wait_ge(in_late, 16 * 7)
                    wait_emptied(pe, ("attnT", b, CC - 1))
                    project(e, [(j * D, j * D + D, [(xT_sb[:, b, c, (2 * half + j) * P:(2 * half + j + 1) * P],
                                                     w_o[:, c, :]) for c in range(CC)]) for j in range(2)])
                elif kind == "x1T":
                    _, b, dc = e
                    pe.wait_ge(ln_done, b + 1)
                    turn(e, [x_sb[:, b, q, dc * P:dc * P + P] for q in range(QT)])
                elif kind == "A":
                    _, p, i = e
                    b, h, q = p // PAIRS, 2 * (p % PAIRS) + i // 4, i % 4
                    if i == 0 and p % 4 == 0:
                        pe.wait_ge(rows_in[b][(p % PAIRS) // 4], 16 * 12)
                        pe.wait_ge(in_const, 16 * 4)
                    if 8 * p + i >= 2:
                        pe.wait_ge(a_max, 8 * p + i - 1)
                    pe.matmul(psA[:, i % 2, :], ops[b][0:SELF_ROWS, 0, h, q * P:q * P + P],
                              ops[b][0:SELF_ROWS, 1, h, :], start=True, stop=True).then_inc(a_full, 1)
                elif kind == "M":
                    p = e[1]
                    pe.wait_ge(init_done, 6)
                    pe.wait_ge(max_parts, p + 1)
                    if p:
                        pe.wait_ge(max_rows, p)
                    for hh in range(2):
                        for q in range(QT):
                            ins = pe.transpose(psT[0:2, hh, q * P:q * P + P], mparts[:, p % 2, hh, q, :],
                                               identb[:, :])
                    ins.then_inc(max_turned, 1)
                elif kind == "B":
                    _, p, i = e
                    b, h, kb = p // PAIRS, 2 * (p % PAIRS) + i // 4, i % 4
                    if i == 0:
                        pe.wait_ge(max_rows, p + 1)
                    if 8 * p + i >= 2:
                        pe.wait_ge(exp_done, 8 * p + i - 1)
                    pe.matmul(psB[:, i % 2, :], ops[b][0:SELF_ROWS, 1, h, kb * P:kb * P + P],
                              ops[b][0:SELF_ROWS, 0, h, :], start=True, stop=True).then_inc(b_full, 1)
                elif kind == "C":
                    _, u, kb = e
                    b, g = u // UNITS, u % UNITS
                    if kb == 0:
                        pe.wait_ge(exp_done, 16 * (u + 1))
                        pe.wait_ge(init_done, 6)
                        if u:
                            pe.wait_ge(outT_ready, u)
                        if g == 0:
                            wait_emptied(pe, ("val", b, 1))
                    for j in range(HG):
                        ins = pe.matmul(psC[32 * j:32 * j + VW, :], v_self[:, b, kb, HG * g + j, :],
                                        pself[:, (HG * u + j) % PRING, kb, :], start=(kb == 0), stop=(kb == KB - 1))
                    if kb == KB - 1:
                        ins.then_inc(c_done, 1)
            for b in range(B):
                wait_emptied(pe, ("xval", b, XKB // 2 - 1))
                pe.wait_ge(kx_in[b], 16 * 13)
                for t, at in tiles(pe, b):
                    for e in job:
                        kind = e[0]
                        if kind == "A":
                            _, g, i = e
                            if g == 0 and i == 0:
                                pe.wait_ge(qx_in[b], at("qx", 16 * 12))
                            if 8 * g + i >= 2:
                                pe.wait_ge(X[b]["a_max"], at("a_max", 8 * g + i - 1))
                            h = HG * g + i // 2
                            pe.matmul(psA[:, i % 2, :], qx[0:SPLIT_ROWS, b, h, :],
                                      kx[b][0:SPLIT_ROWS, h, (i % 2) * S:(i % 2) * S + S], start=True, stop=True)\
                              .then_inc(X[b]["a_full"], 1)
                        elif kind == "M":
                            g = e[1]
                            pe.wait_ge(X[b]["parts"], at("parts", 3 * (g + 1)))
                            if g:
                                pe.wait_ge(X[b]["rows"], at("rows", g))
                            for j in range(HG):
                                ins = pe.transpose(psT[0:2, 0, j * P:j * P + P], xparts[:, j, :], identb[:, :])
                            ins.then_inc(X[b]["turned"], 1)
                        elif kind == "B":
                            _, g, i = e
                            if i == 0:
                                pe.wait_ge(X[b]["rows"], at("rows", g + 1))
                            if 8 * g + i >= 2:
                                pe.wait_ge(X[b]["exp"], at("exp", 8 * g + i - 1))
                            h = HG * g + i // 2
                            for k in range(4):
                                kb = 4 * (i % 2) + k
                                ins = pe.matmul(psB[:, i % 2, k * P:k * P + P],
                                                kx[b][0:CROSS_ROWS, h, kb * P:kb * P + P],
                                                qx[0:CROSS_ROWS, b, h, :], start=True, stop=True)
                            ins.then_inc(X[b]["b_full"], 1)
                        elif kind == "C":
                            _, g, kb = e
                            if kb == 0:
                                pe.wait_ge(X[b]["exp"], at("exp", 8 * (g + 1)))
                                if g:
                                    pe.wait_ge(X[b]["outT"], at("outT", g))
                            for j in range(HG):
                                ins = pe.matmul(psC[32 * j:32 * j + VW, 0:P], v_cross[:, b, kb, HG * g + j, :],
                                                pcross[:, g % 2, j, kb, :], start=(kb == 0), stop=(kb == XKB - 1))
                            if kb == XKB - 1:
                                ins.then_inc(X[b]["c_done"], 1)
                        elif kind == "norm":
                            g = e[1]
                            pe.wait_ge(X[b]["outT"], at("outT", g + 1))
                            if g >= 2:
                                pe.wait_ge(X[b]["n_done"], at("n_done", 2 * (g - 1)))
                            pe.transpose(psN[:, g % 2, 0:P], outT[:, 0:P], identf[:, :]).then_inc(X[b]["n_full"], 1)
            pe.wait_ge(in_ffn, 16 * 3)
            for b in range(B):
                pe.wait_ge(ln_done, B + b + 1)
                if b:
                    pe.wait_ge(f_dve, 2 * b)
                for cc in range(CC):
                    for q in range(QT):
                        ins = pe.transpose(psN[:, cc, q * P:q * P + P], x_sb[:, b, q, cc * P:cc * P + P],
                                           identf[:, :])
                    ins.then_inc(f_full, 1)
                pe.wait_ge(mix_done, 2 * b + 1)
                for dc in range(CC):
                    for cc in range(CC):
                        ins = pe.matmul(psN[:, dc, :], w_k2[:, cc, dc * P:dc * P + P], xk[:, b, cc, :],
                                        start=(cc == 0), stop=(cc == CC - 1))
                    ins.then_inc(f_full, 1)
                pe.wait_ge(mix_done, 2 * b + 2)
                for half in range(2):
                    pe.wait_ge(act_step, 4 * b + 2 * half + 2)
                    for j in range(2):
                        q = 2 * half + j
                        for cc in range(CC):
                            ins = pe.matmul(psN[:, half, j * D:j * D + D], xr[:, b, cc, q * P:q * P + P],
                                            w_r[:, cc, :], start=(cc == 0), stop=(cc == CC - 1))
                    ins.then_inc(f_full, 1)
                for half in range(2):
                    pe.wait_ge(f_act, 4 * b + 2 + half + 1)
                    for j in range(2):
                        q = 2 * half + j
                        for cc in range(CC):
                            ins = pe.matmul(psN[:, half, j * D:j * D + D], kact[:, cc, q * P:q * P + P],
                                            w_v2[:, cc, :], start=(cc == 0), stop=(cc == CC - 1))
                    ins.then_inc(f_full, 1)


def kernel(**inputs):
    import ml_dtypes
    import numpy as np
    import concourse.bacc as bacc
    from concourse.bass_utils import run_bass_kernel_spmd as run

    def arr(name):
        return np.asarray(inputs[name])

    def by_head(b):
        return np.ascontiguousarray(b.reshape(CC, H // CC, HD).transpose(2, 1, 0).reshape(P, CC))

    def columns(w):
        return np.ascontiguousarray(w.reshape(-1, CC, H // CC, HD).transpose(0, 1, 3, 2).reshape(-1, D))

    def T(a):
        return np.ascontiguousarray(np.swapaxes(a, -1, -2))

    slopes = (np.float32(1) / np.float32(2) ** (np.arange(H, dtype=np.float32) / np.float32(H))).astype(np.float32)
    term = slopes[:, None] * np.arange(S, dtype=np.float32)[None, :]
    hi = term.astype(ml_dtypes.bfloat16)
    mid = (term - hi.astype(np.float32)).astype(ml_dtypes.bfloat16)
    low = (term - hi.astype(np.float32) - mid.astype(np.float32)).astype(ml_dtypes.bfloat16)
    one = np.ones_like(hi)
    k_rows = np.stack([one, one, hi, mid, low])
    q_rows = np.stack([0 * one, 0 * one, one, one, one])
    kvT = T(arr("L0_xattn_Wkv"))
    data = {
        "x": arr("x"), "xT": T(arr("x")), "ctxT": T(arr("ctx_768")), "mask": arr("mask_BxS_bk0"),
        "wq": columns(arr("L0_attn_Wq")), "bq": by_head(arr("L0_attn_bq")), "wk": columns(arr("L0_attn_Wk")),
        "bk": by_head(arr("L0_attn_bk")), "wv": arr("L0_attn_Wv"), "bv": arr("L0_attn_bv"), "wo": arr("L0_attn_Wo"),
        "bo": arr("L0_attn_bo"), "xwqT": columns(T(arr("L0_xattn_Wq"))), "xwkvT": np.concatenate([columns(kvT[:, :D]), kvT[:, D:]], axis=1),
        "wrT": T(arr("L0_ffn_W_r")), "wkT": T(arr("L0_ffn_W_k")), "wvT": T(arr("L0_ffn_W_v")),
        "mur": T(arr("L0_ffn_mu_r").reshape(CC, P)), "muk": T(arr("L0_ffn_mu_k").reshape(CC, P)),
        "k_rows": k_rows, "q_rows": q_rows, "ident": np.eye(P, dtype=np.float32),
    }
    nc = bacc.Bacc("TRN2", target_bir_lowering=False, num_devices=1)
    arrays, args = {}, []
    for name, a in data.items():
        a = np.ascontiguousarray(a)
        arrays[f"in_{name}"] = a
        args.append(nc.dram_tensor(f"in_{name}", a.shape, mybir.dt.from_np(a.dtype), kind="ExternalInput").ap())
    args.append(nc.dram_tensor("out_x", (B, S, D), F32, kind="ExternalOutput").ap())
    decoder_layer(nc, *args)
    return run(nc, [arrays], core_ids=[0]).results[0]["out_x"]
```

```python
from contextlib import ExitStack

import concourse.bass as bass
from concourse import mybir

F32 = mybir.dt.float32
BF16 = mybir.dt.bfloat16
I32 = mybir.dt.int32
U8 = mybir.dt.uint8
ALU = mybir.AluOpType
ACT = mybir.ActivationFunctionType
AX = mybir.AxisListType.X

P = 128
B, S, D = 2, 512, 256
H, HD = 16, 16
S2, DC = 1024, 192
CC = D // P
XC = 96
QT = S // P
KB = S // P
XKB = S2 // P
HG = 4
UNITS = H // HG
PAIRS = H // 2
VW = HD + 1
EPS = 1e-5
QSCALE = float(HD) ** -0.5
Q_PARTS = (0, 0, 0, 1, 1, 2)
K_PARTS = (2, 0, 1, 0, 1, 0)
SPLIT_ROWS = HD * len(Q_PARTS)
MAX_ROW = SPLIT_ROWS
MAX_ROWS = 2 * HG
CROSS_ROWS = SPLIT_ROWS + MAX_ROWS
SELF_ROWS = CROSS_ROWS + 3
PRING = 6


SELF_A = B * PAIRS
CROSS_A = B * UNITS
SELF_U = B * UNITS
LAST = QT - 1


def plan():
    at_step = list(range(SELF_A + UNITS)) + [None, None] + list(range(SELF_A + UNITS, SELF_A + CROSS_A))
    when = {a: s for s, a in enumerate(at_step) if a is not None}
    last_step = max(when.values()) + 3

    def proj(w, b, halves=1):
        return [("proj", w, b, dc, half) for dc in range(CC) for half in range(halves)]

    def two(kind, b):
        return [(kind, b, n) for n in range(2)]

    order = [("proj", "q", 0, 0, 0), ("proj", "k", 0, 0, 0), ("val", 0, 0), ("val", 0, 1),
             ("proj", "q", 0, 1, 0), ("proj", "k", 0, 1, 0)]
    xval = [[("xval", b, n) for n in range(XKB // 2)] for b in range(B)]
    early = ([("proj", "q", 1, 0, 0), ("proj", "k", 1, 0, 0), ("bias", 0), ("proj", "q", 1, 1, 0),
              ("proj", "k", 1, 1, 0), ("bias", 1), ("ctxsum", 0)] + proj("x", 0, 2) + xval[0] + [("mean", 0)]
             + two("val", 1) + [("ctxsum", 1)] + proj("x", 1, 2))
    first = when[SELF_A - 1] + 3
    placed = {
        first - 7: {1: two("attnT", 0), 5: two("wo", 0)},
        first - 6: {1: [("lnA", 1, 0)], 5: [("lnB", 1, 0)]},
        first - 5: {1: two("x1T", 0), 5: proj("c", 0), 7: [("qxread", 0)]},
        first - 4: {1: [("fill", 0)]},
        first + 1: {0: two("attnT", 1), 2: [xval[1][0]], 3: two("wo", 1), 5: [("lnA", 1, 1)], 6: [xval[1][1]]},
        first + 2: {0: [("lnB", 1, 1), xval[1][2]], 1: two("x1T", 1), 2: [xval[1][3]], 4: proj("c", 1),
                    5: [("qxread", 1)], 6: [("mean", 1)]},
        first + 3: {1: [("fill", 1)]},
        first + 4: {6: [("select", 0), ("rare", 0)], 7: [("lnA", 2, 0)]},
        first + 5: {2: [("lnB", 2, 0)], 4: two("x2T", 0), 5: [("mixA", 0)], 7: [("mixB", 0)]},
        first + 6: {1: two("fk", 0), 4: two("fr", 0), 7: [("fv", 0, 0)]},
        first + 7: {1: [("fv", 0, 1)], 2: [("lnA", 3, 0)], 6: [("lnB", 3, 0)]},
    }
    for s in range(last_step + 1):
        rate = (0, 2, 4, 6) if s < 2 else (1, 5)
        for i in range(8):
            if s < len(at_step) and at_step[s] is not None:
                order.append(("A", at_step[s], i))
            a = next((a for a in when if when[a] == s - 2), None)
            if a is not None:
                order.append(("B", a, i))
            m = next((a for a in when if when[a] == s - 1), None)
            if i == 3 and m is not None:
                order.append(("M", m))
            if i in rate and early:
                order.append(early.pop(0))
                while order[-1][0] in ("bias", "ctxsum"):
                    order.append(early.pop(0))
            order += placed.get(s, {}).get(i, [])
            if s >= 4 and s % 2 == 0 and (s - 4) // 2 < SELF_U and 2 <= i < 2 + KB:
                u = (s - 4) // 2
                order.append(("C", u, i - 2))
                if i == 1 + KB:
                    order += [("O", u)]
            if s >= 4 and s % 2 == 0 and (s - 4) // 2 < SELF_U and i == 6:
                order.append(("norm", (s - 4) // 2))
                if s == PAIRS + 2:
                    order.append(("kxread", 0))
            c = next((a for a in when if when[a] == s - 3 and a >= SELF_A), None)
            if c is not None:
                u = SELF_U + c - SELF_A
                if i < 4:
                    order += [("C", u, 2 * i), ("C", u, 2 * i + 1)]
                if i == 3:
                    order.append(("O", u))
                if i == 5:
                    order.append(("norm", u))
        if s == when[SELF_A - 1] + 2:
            order.append(("kxread", 1))
    assert not early
    b = B - 1
    order += [("select", b), ("rare", b), ("lnA", 2, b), ("lnB", 2, b)] + two("x2T", b) + [("mixA", b), ("mixB", b)]
    order += two("fk", b) + two("fr", b) + two("fv", b) + [("lnA", 3, b), ("lnB", 3, b)]
    return order


def decoder_layer(nc, x, xT, ctxT, mask, wqk, cols, wv, bv, wo, bo, xwqT, xwkvT, wrT, wkT, wvT, k_rows, q_rows, ident,
                  out):
    order = plan()
    items = [e for e in order if e[0] in ("proj", "val", "xval", "mean", "norm", "attnT", "wo", "x1T", "x2T", "fk",
                                          "fr", "fv")]
    nth = {e: n for n, e in enumerate(items)}
    ON_ACT = ("xval", "mean", "attnT", "x1T", "x2T", "fk", "fr")
    rank = {}
    for e in items:
        rank[e] = sum(1 for f in items[:nth[e] + 1] if (f[0] in ON_ACT) == (e[0] in ON_ACT))
    splits = [e for e in items if e[0] == "proj"]
    split_no = {e: k for k, e in enumerate(splits)}
    ln_no = {e[1:]: n + 1 for n, e in enumerate(e for e in order if e[0] == "lnA")}

    def fast(e):
        return e[1] == "c" or (e[1] in "qk" and e[2] == 0)

    split_rank = {e: sum(1 for f in splits[:split_no[e] + 1] if fast(f) == fast(e)) for e in splits}

    ctx = ExitStack()
    with ctx:
        def sb(name, shape, dt=F32):
            return ctx.enter_context(nc.sbuf_tensor(name, shape, dt))

        def ps(name, shape, dt=F32):
            return ctx.enter_context(nc.psum_tensor(name, shape, dt))

        def sem(name):
            return ctx.enter_context(nc.semaphore(name))

        ops = [sb(f"ops{b}", [P, 2, H, S], BF16) for b in range(B)]
        kx = [ops[b][:, :, :, :].rearrange("p a h t -> p (a h t)").rearrange("p (h t) -> p h t", h=H) for b in range(B)]
        probs = sb("probs", [P, PRING * KB * S])
        pself = probs[:, :].rearrange("p (r k t) -> p r k t", r=PRING, k=KB)
        pcross = probs[:, :].rearrange("p (u j k t) -> p u j k t", u=3, j=HG, k=XKB)
        RARE = 2
        v_self = sb("v_self", [P, B * KB * H * VW])
        vs = v_self[:, :].rearrange("p (b k h d) -> p b k h d", b=B, k=KB, h=H)
        v_cross = sb("v_cross", [P, B, XKB, H, VW])
        x_sb = sb("x_sb", [P, B, QT, D])
        xT_sb = sb("xT_sb", [P, B, CC, S])
        ctx_sb = sb("ctx_sb", [P, 2, S2])
        attn = sb("attn", [P, B, QT, D])
        w_qk = sb("w_qk", [P, CC, 2 * D])
        w_v, w_o, w_xq = (sb(f"w{n}", [P, CC, D]) for n in ("v", "o", "xq"))
        w_kv = sb("w_kv", [XC, 2, 2 * D])
        qx0 = sb("qx0", [P, H, P], BF16)
        qx = [qx0[:, :, :], w_qk[:, :, :].rearrange("p c n -> p (c n)").bitcast(BF16).rearrange("p (h t) -> p h t", h=H)]
        q32 = sb("q32", [P, 2, S])
        parts = sb("parts", [P, 2, 3, S], BF16)
        outT = sb("outT", [P, S])
        identf = sb("identf", [P, P])
        identb = sb("identb", [P, P], BF16)
        cols_sb = sb("cols_sb", [P, 4, CC])
        bq_c, bk_c, mur_c, muk_c = (cols_sb[:, n, :] for n in range(4))
        bv_r, bo_r = sb("bv_r", [P, D]), sb("bo_r", [P, D])
        om_r, om_k = sb("om_r", [P, CC]), sb("om_k", [P, CC])
        meanv = sb("meanv", [P, B, D])
        csum = sb("csum", [XC, 2])
        csum_r = sb("csum_r", [XC, 2, P])
        mx = sb("mx", [P, 2, 8])
        mparts = sb("mparts", [P, 2, QT, HG, 2], BF16)
        rden = sb("rden", [P, QT, HG])
        stats = sb("stats", [P, QT, 6])
        mv = sb("mv", [P, QT, 2])
        ve = sb("ve", [P, QT])
        rstd = sb("rstd", [P, QT])
        nhalf = sb("nhalf", [P, QT])
        minus = sb("minus", [P, HG])
        mask_q = sb("mask_q", [P, B, QT], U8)
        mask_row = sb("mask_row", [1, B, QT, P], U8)
        live = sb("live", [1, B, QT])
        weight = sb("weight", [1, B, QT])
        behind = sb("behind", [1, B])
        count_i = sb("count_i", [1, B], I32)
        xm = sb("xm", [P, HG, 2])
        xmax = sb("xmax", [P, HG])
        xres = sb("xres", [P, HG])
        xparts = sb("xparts", [P, HG, 2], BF16)
        xrd = sb("xrd", [P, HG])
        cmax = sb("cmax", [P, HG])
        tile_att, tile_rare, tile_sel = w_v, bv_r[:, :], bo_r[:, :]
        mcur = sb("mcur", [P, 1], U8)
        gate_pad = sb("gate_pad", [P, 1])
        w_r, w_k2, w_v2 = (v_self[:, n * CC * D:(n + 1) * CC * D].rearrange("p (c d) -> p c d", c=CC) for n in range(3))
        room = ops[0][:, :, :, :].rearrange("p a h t -> p (a h t)").bitcast(F32)
        cursor = [0]

        def in_room(t):
            n = B * CC * t
            a = room[:, cursor[0]:cursor[0] + n].rearrange("p (b c t) -> p b c t", b=B, c=CC)
            cursor[0] += n
            return a
        x2T, xr, xk = in_room(S + 1), in_room(S), in_room(S)

        psA = ps("psA", [P, 2, S])
        psB = ps("psB", [P, 2, S])
        psC = ps("psC", [P, S])
        psT = ps("psT", [P, 2, S], BF16)
        psN = ps("psN", [P, 2, S])

        GROUPS = len(Q_PARTS)
        scr = {w: nc.dram_tensor(f"scr_{w}", [B, CC, GROUPS, HD, H // CC, S2 if w == "x" else S], BF16).ap()
               for w in "qkxc"}

        in_qk, in_ident, in_v, in_ctx, in_late, in_mask, in_ffn = (
            sem(n) for n in ("in_qk", "in_ident", "in_v", "in_ctx", "in_late", "in_mask", "in_ffn"))
        in_const = [sem(f"in_const{b}") for b in range(B)]
        init_done = sem("init_done")
        INIT = 7
        bank_full = sem("bank_full")
        dve_emptied, act_emptied = sem("dve_emptied"), sem("act_emptied")
        dve_split, pool_split = sem("dve_split"), sem("pool_split")
        scr_written = [sem(f"scr_written{n}") for n in range(2)]
        rows_in = [[sem(f"rows_in{b}{dc}") for dc in range(CC)] for b in range(B)]
        kx_in = [sem(f"kx_in{b}") for b in range(B)]
        qx_in = [sem(f"qx_in{b}") for b in range(B)]
        csum_ready = sem("csum_ready")
        a_full, a_max = sem("a_full"), sem("a_max")
        max_parts, max_turned, max_rows = sem("max_parts"), sem("max_turned"), sem("max_rows")
        b_full, exp_done = sem("b_full"), sem("exp_done")
        c_done, outT_ready = sem("c_done"), sem("outT_ready")
        var_ready, rstd_ready, ln_done = sem("var_ready"), sem("rstd_ready"), sem("ln_done")
        residual, filled = sem("residual"), sem("filled")
        dve_step, pool_step = sem("dve_step"), sem("pool_step")
        count_ready = sem("count_ready")
        passed = sem("passed")
        gate = [sem(f"gate{b}") for b in range(B)]
        rare_over = [sem(f"rare_over{b}") for b in range(B)]
        X = [{n: sem(f"x{n}{b}") for n in ("a_full", "a_max", "max2", "parts", "turned", "rows", "b_full", "exp", "c_done",
                                           "outT", "n_full", "n_done")} for b in range(B)]
        XTOT = {"a_full": 32, "a_max": 32, "parts": 12, "max2": 4, "turned": 4, "rows": 4, "b_full": 32, "exp": 32, "c_done": 4,
                "outT": 4, "n_full": 4, "n_done": 11, "qx": 16 * CC}
        om_ready, pad_ready, mix_prev, mix_done, squared, stored = (
            sem(n) for n in ("om_ready", "pad_ready", "mix_prev", "mix_done", "squared", "stored"))

        def bank(e):
            return psN[:, nth[e] % 2, :]

        def wait_emptied(eng, e):
            eng.wait_ge(act_emptied if e[0] in ON_ACT else dve_emptied, rank[e])

        def wait_split(eng, e):
            eng.wait_ge(dve_split if fast(e) else pool_split, split_rank[e])

        def wait_written(eng, k):
            eng.wait_ge(scr_written[k % 2], 16 * 3 * (k // 2 + 1))

        def cross(a):
            return (a - SELF_A) // UNITS, (a - SELF_A) % UNITS

        job = []
        for s in range(UNITS + 2):
            for i in range(8):
                if s < UNITS:
                    job.append(("A", s, i))
                if i < 4 and s >= 2:
                    job += [("C", s - 2, 2 * i), ("C", s - 2, 2 * i + 1)]
                if i == 3:
                    if s >= 2:
                        job += [("O", s - 2), ("norm", s - 2)]
                    if 1 <= s <= UNITS:
                        job.append(("M", s - 1))
                if i >= 4 and 1 <= s <= UNITS:
                    job.append(("B", s - 1, i - 4))
            if 1 <= s <= UNITS:
                job += [("B", s - 1, i) for i in range(4, 8)]

        def rare_tiles(eng, b, first=None):
            eng.wait_ge(count_ready, 1)
            count = eng.value_load(count_i[0:1, b:b + 1], min_val=0, max_val=QT - 1)
            with eng.If(count > 0):
                if first:
                    first()
                with eng.Fori(0, count) as n:
                    def at(name, c):
                        return n * XTOT[name] + c
                    eng.wait_ge(gate[b], n + 1)
                    eng.sem_inc(passed, 1)
                    yield (LAST - 1) - n, at
                if first:
                    eng.memset(gate_pad[:, :], 0.0).then_inc(rare_over[b], 1)
                eng.wait_ge(rare_over[b], 1)

        block = ctx.enter_context(nc.Block())

        @block.sync
        def _(sp):
            def load(dst, src, s):
                sp.dma_start(dst, src).then_inc(s, 16)

            def wide(w):
                return w.rearrange("(c p) n -> p c n", p=P)

            def stacked(w, b, dc):
                return scr[w][b, dc].rearrange("g d h t -> (g d) h t")

            load(xT_sb[:, 0, :, :], xT[0].rearrange("(c p) t -> p c t", p=P), in_qk)
            load(w_qk[:, :, :], wide(wqk), in_qk)
            load(cols_sb[:, :, :].rearrange("p n c -> p (n c)"), cols, in_qk)
            load(w_v[:, :, :], wide(wv), in_v)
            load(bv_r[:, :], bv.rearrange("(a n) -> a n", a=1).broadcast_to([P, D]), in_v)
            load(xT_sb[:, 1, :, :], xT[1].rearrange("(c p) t -> p c t", p=P), in_v)
            load(ctx_sb[0:XC, :, :], ctxT[0].rearrange("(c p) t -> p c t", p=XC), in_ctx)
            load(w_kv[:, :, :], xwkvT.rearrange("(c p) n -> p c n", p=XC), in_ctx)
            for e in order:
                if e[0] == "proj":
                    _, w, b, dc, half = e
                    k = split_no[e]
                    cut = slice(half * S, half * S + S)
                    wait_split(sp, e)
                    places = scr[w][b, dc].rearrange("g d h t -> (d h) g t")
                    for j in range(3):
                        met = (slice(0, 3), slice(3, 5), slice(5, 6)) if w in "qc" else \
                              (slice(1, 6, 2), slice(2, 5, 2), slice(0, 1))
                        dst = places[:, met[j], cut]
                        sp.dma_start(dst, parts[:, k % 2, j, :].unsqueeze(1).broadcast_to([P, dst.shape[1], S]))\
                          .then_inc(scr_written[k % 2], 16)
                    if w == "k":
                        for op, split in ((0, k - 1), (1, k)):
                            wait_written(sp, split)
                            load(ops[b][0:SPLIT_ROWS, op, 8 * dc:8 * dc + 8, :], stacked("qk"[op], b, dc), rows_in[b][dc])
                elif e == ("ctxsum", 1):
                    sp.wait_ge(bank_full, nth[("mean", 0)] + 1)
                    sp.wait_ge(csum_ready, 1)
                    load(ctx_sb[0:XC, :, :], ctxT[1].rearrange("(c p) t -> p c t", p=XC), in_ctx)
                elif e[0] == "kxread":
                    b = e[1]
                    last = split_no[("proj", "x", b, CC - 1, 1)]
                    wait_written(sp, last)
                    wait_written(sp, last - 1)
                    sp.wait_ge(b_full, 8 * PAIRS * (b + 1))
                    for dc in range(CC):
                        load(kx[b][0:SPLIT_ROWS, 8 * dc:8 * dc + 8, :], stacked("x", b, dc), kx_in[b])
                        load(kx[b][MAX_ROW:CROSS_ROWS, :, dc * S:dc * S + S], k_rows[0:MAX_ROWS, :, :], kx_in[b])
                elif e[0] == "qxread":
                    b = e[1]
                    last = split_no[("proj", "c", b, CC - 1, 0)]
                    wait_written(sp, last)
                    wait_written(sp, last - 1)
                    for dc in range(CC):
                        load(qx[b][0:SPLIT_ROWS, 8 * dc:8 * dc + 8, :], stacked("c", b, dc)[:, :, LAST * P:S], qx_in[b])
                    if b == B - 1:
                        sp.wait_ge(c_done, SELF_U)
                        for dst, src in ((w_k2, wkT), (w_r, wrT), (w_v2, wvT)):
                            load(dst, wide(src), in_ffn)
                elif e[0] == "rare":
                    b = e[1]
                    for t, at in rare_tiles(sp, b):
                        for dc in range(CC):
                            load(qx[b][0:SPLIT_ROWS, 8 * dc:8 * dc + 8, :], stacked("c", b, dc)[:, :, bass.ts(t, P)],
                                 qx_in[b])
                elif e[0] == "lnB" and e[1] == 3:
                    sp.wait_ge(ln_done, ln_no[e[1:]])
                    load(out[e[2]].rearrange("(q p) d -> p q d", p=P), x_sb[:, e[2], :, :], stored)
            sp.wait_ge(stored, 16 * B)

        @block.gpsimd
        def _(pool):
            steps = [0]

            def step(ins):
                steps[0] += 1
                ins.then_inc(pool_step, 1)
                pool.wait_ge(pool_step, steps[0])

            pool.memset(mparts[:, :, :, :, :], 0.0).then_inc(init_done, 1)
            pool.memset(vs[:, :, :, :, HD:VW], 1.0).then_inc(init_done, 1)
            pool.memset(v_cross[:, :, :, :, HD:VW], 1.0).then_inc(init_done, 1)
            pool.memset(minus[:, :], -1.0).then_inc(init_done, 1)
            pool.memset(nhalf[:, :], -0.5).then_inc(init_done, 1)
            for e in order:
                if e[0] == "bias":
                    b = e[1]
                    pool.wait_ge(in_late, 16 * 5)
                    for q in range(QT):
                        ins = pool.tensor_tensor(x_sb[:, b, q, :], x_sb[:, b, q, :], bo_r[:, :], ALU.add)
                    ins.then_inc(residual, 1)
                elif e[0] == "proj" and not fast(e):
                    k = split_no[e]
                    pool.wait_ge(dve_emptied, rank[e])
                    if k >= 2:
                        wait_written(pool, k - 2)
                    v, pt = q32[:, k % 2, :], parts[:, k % 2, :, :]
                    step(pool.tensor_copy(pt[:, 0, :], v))
                    step(pool.tensor_tensor(v, v, pt[:, 0, :], ALU.subtract))
                    step(pool.tensor_copy(pt[:, 1, :], v))
                    pool.tensor_tensor(pt[:, 2, :], v, pt[:, 1, :], ALU.subtract).then_inc(pool_split, 1)
                elif e[0] == "lnA":
                    pool.wait_ge(init_done, INIT)
                    pool.wait_ge(var_ready, ln_no[e[1:]])
                    pool.tensor_tensor(rstd[:, :], ve[:, :], nhalf[:, :], ALU.pow).then_inc(rstd_ready, 1)
                elif e[0] == "rare":
                    b = e[1]
                    for t, at in rare_tiles(pool, b):
                        for f in job:
                            if f[0] == "M":
                                g = f[1]
                                pool.wait_ge(X[b]["max2"], at("max2", g + 1))
                                if g >= 1:
                                    pool.wait_ge(X[b]["turned"], at("turned", g))
                                pool.tensor_tensor(xparts[:, :, 0], xmax[:, :], minus[:, :], ALU.mult)\
                                    .then_inc(X[b]["parts"], 1)
                                pool.wait_ge(X[b]["parts"], at("parts", 3 * g + 1))
                                pool.tensor_tensor(xres[:, :], xmax[:, :], xparts[:, :, 0], ALU.add)\
                                    .then_inc(X[b]["parts"], 1)
                                pool.wait_ge(X[b]["parts"], at("parts", 3 * g + 2))
                                pool.tensor_tensor(xparts[:, :, 1], xres[:, :], minus[:, :], ALU.mult)\
                                    .then_inc(X[b]["parts"], 1)

        @block.scalar
        def _(act):
            act.dma_start(identf[:, :], ident).then_inc(in_ident, 16)
            act.dma_start(mask_row[0:1, :, :, :], mask.rearrange("(a b) (q p) -> a b q p", a=1, p=P))\
               .then_inc(in_mask, 16)
            for b in range(B):
                act.dma_start(ops[b][MAX_ROW:SELF_ROWS, 0, :, :], q_rows).then_inc(in_const[b], 16)
                act.dma_start(ops[b][MAX_ROW:SELF_ROWS, 1, :, :], k_rows).then_inc(in_const[b], 16)
            with nc.allow_non_contiguous_dma(reason="one byte for each query"):
                act.dma_start(mask_q[:, :, :], mask.rearrange("b (q p) -> p b q", p=P)).then_inc(in_mask, 16)
            act.dma_start(x_sb[:, 0, :, :], x[0].rearrange("(q p) d -> p q d", p=P)).then_inc(in_late, 16)
            act.dma_start(x_sb[:, 1, :, :], x[1].rearrange("(q p) d -> p q d", p=P)).then_inc(in_late, 16)
            act.dma_start(bo_r[:, :], bo.rearrange("(a n) -> a n", a=1).broadcast_to([P, D])).then_inc(in_late, 16)
            act.dma_start(w_o[:, :, :], wo.rearrange("(c p) n -> p c n", p=P)).then_inc(in_late, 16)
            act.dma_start(w_xq[:, :, :], xwqT.rearrange("(c p) n -> p c n", p=P)).then_inc(in_late, 16)
            act.wait_ge(in_ident, 16)
            act.activation(identb[:, :], identf[:, :], ACT.Copy).then_inc(init_done, 1)
            for e in order:
                kind = e[0]
                if kind == "B":
                    _, a, i = e
                    n = 8 * a + i
                    if a < SELF_A:
                        head = 2 * a + i // 4
                        if i % 4 == 0 and head >= PRING:
                            act.wait_ge(c_done, (head - PRING) // HG + 1)
                        dst = pself[:, head % PRING, i % 4, :]
                    else:
                        u = a - SELF_A + SELF_U
                        if i == 0:
                            act.wait_ge(c_done, u - 1)
                        dst = pcross[:, (u + 1) % 2, i // 2, 4 * (i % 2):4 * (i % 2) + 4, :]\
                            .rearrange("p k t -> p (k t)")
                    act.wait_ge(b_full, n + 1)
                    act.activation(dst, psB[:, n % 2, :], ACT.Exp).then_inc(exp_done, 1)
                elif kind == "M":
                    a = e[1]
                    act.wait_ge(max_turned, a + 1)
                    if a < SELF_A:
                        b, h = a // PAIRS, 2 * (a % PAIRS)
                        act.activation(ops[b][MAX_ROW:CROSS_ROWS, 0, h:h + 2, :],
                                       psT[0:MAX_ROWS, a % 2, :].unsqueeze(1).broadcast_to([MAX_ROWS, 2, S]), ACT.Copy)\
                           .then_inc(max_rows, 1)
                    else:
                        b, g = cross(a)
                        act.activation(qx[b][MAX_ROW:CROSS_ROWS, HG * g:HG * g + HG, :],
                                       psT[0:MAX_ROWS, a % 2, 0:P].unsqueeze(1).broadcast_to([MAX_ROWS, HG, P]),
                                       ACT.Copy).then_inc(max_rows, 1)
                elif kind == "O":
                    u = e[1]
                    act.wait_ge(c_done, u + 1)
                    if u >= 1:
                        act.wait_ge(bank_full, nth[("norm", u - 1)] + 1)
                    w = S if u < SELF_U else P
                    act.activation(outT[:, 0:w], psC[:, 0:w], ACT.Copy).then_inc(outT_ready, 1)
                elif kind in ON_ACT:
                    act.wait_ge(bank_full, nth[e] + 1)
                    bk_ = bank(e)
                    if kind == "xval":
                        _, b, i = e
                        for j in range(2):
                            ins = act.activation(v_cross[:, b, 2 * i + j, :, 0:HD],
                                                 bk_[:, j * D:j * D + D].rearrange("p (h d) -> p h d", h=H), ACT.Copy)
                    elif kind == "mean":
                        ins = act.activation(meanv[:, e[1], :], bk_[:, 0:D], ACT.Copy)
                    elif kind == "x2T":
                        ins = act.activation(x2T[:, e[1], e[2], 1:S + 1], bk_, ACT.Copy)
                    elif kind == "fr":
                        ins = act.activation(attn[:, e[1], 2 * e[2]:2 * e[2] + 2, :].rearrange("p q d -> p (q d)"), bk_,
                                             ACT.Tanh, scale=0.5)
                    else:
                        ins = act.activation(xT_sb[:, e[1], e[2], :], bk_, ACT.Relu if kind == "fk" else ACT.Copy)
                    ins.then_inc(act_emptied, 1)
                elif kind == "fill":
                    b = e[1]
                    act.wait_ge(bank_full, nth[("attnT", b, CC - 1)] + 1)
                    wait_emptied(act, ("mean", b))
                    act.activation(attn[:, b, :, :], meanv[:, b, :].unsqueeze(1).broadcast_to([P, QT, D]), ACT.Copy)\
                       .then_inc(filled, 1)
                elif kind == "mixA":
                    b = e[1]
                    wait_emptied(act, ("x2T", b, CC - 1))
                    act.wait_ge(om_ready, 2)
                    act.wait_ge(pad_ready, 1)
                    for om, mixed in ((om_k, xk), (om_r, xr)):
                        for cc in range(CC):
                            act.activation(mixed[:, b, cc, :], x2T[:, b, cc, 0:S], ACT.Copy, scale=om[:, cc:cc + 1])\
                               .then_inc(mix_prev, 1)
                elif kind == "rare":
                    b = e[1]
                    for t, at in rare_tiles(act, b):
                        for f in job:
                            if f[0] == "B":
                                _, g, i = f
                                act.wait_ge(X[b]["b_full"], at("b_full", 8 * g + i + 1))
                                if g >= 1 and i == 0:
                                    act.wait_ge(X[b]["c_done"], at("c_done", g))
                                act.activation(pcross[:, RARE, i // 2, 4 * (i % 2):4 * (i % 2) + 4, :]
                                               .rearrange("p k t -> p (k t)"), psB[:, i % 2, :], ACT.Exp)\
                                   .then_inc(X[b]["exp"], 1)
                            elif f[0] == "M":
                                g = f[1]
                                act.wait_ge(X[b]["turned"], at("turned", g + 1))
                                act.activation(qx[b][MAX_ROW:CROSS_ROWS, HG * g:HG * g + HG, :],
                                               psT[0:MAX_ROWS, 0, 0:P].unsqueeze(1).broadcast_to([MAX_ROWS, HG, P]),
                                               ACT.Copy).then_inc(X[b]["rows"], 1)
                            elif f[0] == "O":
                                g = f[1]
                                act.wait_ge(X[b]["c_done"], at("c_done", g + 1))
                                if g >= 1:
                                    act.wait_ge(X[b]["n_full"], at("n_full", g))
                                act.activation(outT[:, 0:P], psC[:, 0:P], ACT.Copy).then_inc(X[b]["outT"], 1)

        @block.vector
        def _(dve):
            steps = [0]

            def step(ins):
                steps[0] += 1
                ins.then_inc(dve_step, 1)
                dve.wait_ge(dve_step, steps[0])

            dve.memset(psC[:, :], 0.0).then_inc(init_done, 1)
            for q in range(QT):
                ins = dve.memset(weight[0:1, :, q:q + 1], float(QT - 1 - q))
            dve.wait_ge(in_mask, 32)
            step(dve.tensor_reduce(live[0:1, :, :], mask_row[0:1, :, :, :], AX, ALU.max))
            step(dve.tensor_tensor(live[0:1, :, :], live[0:1, :, :], weight[0:1, :, :], ALU.mult))
            step(dve.tensor_reduce(behind[0:1, :], live[0:1, :, :], AX, ALU.max))
            dve.tensor_scalar(count_i[0:1, :], behind[0:1, :], 0.0, None, ALU.add).then_inc(count_ready, 1)
            dve.wait_ge(in_qk, 16 * 3)
            dve.tensor_scalar(om_r[:, :], mur_c, -1.0, 1.0, ALU.mult, ALU.add).then_inc(om_ready, 1)
            dve.tensor_scalar(om_k[:, :], muk_c, -1.0, 1.0, ALU.mult, ALU.add).then_inc(om_ready, 1)
            for at_e, e in enumerate(order):
                kind = e[0]
                if kind == "A":
                    _, a, i = e
                    n = 8 * a + i
                    if i == 0 and a >= 2:
                        dve.wait_ge(max_parts, a - 1)
                    dve.wait_ge(a_full, n + 1)
                    dve.tensor_reduce(mx[:, a % 2, i:i + 1], psA[:, n % 2, :], AX, ALU.max).then_inc(a_max, 1)
                elif kind == "M":
                    a = e[1]
                    m = mx[:, a % 2, :].rearrange("p (j q) -> p j q", j=2 if a < SELF_A else HG)
                    dve.wait_ge(a_max, 8 * (a + 1))
                    if a < 2:
                        dve.wait_ge(init_done, INIT)
                    else:
                        dve.wait_ge(max_turned, a - 1)
                    if a < SELF_A:
                        j = 2 * (a % 2)
                        o = [mparts[:, a % 2, :, j:j + 2, part].rearrange("p q j -> p j q") for part in range(2)]
                    else:
                        dve.wait_ge(max_parts, a)
                        step(dve.tensor_reduce(cmax[:, :], m, AX, ALU.max))
                        m = cmax[:, :]
                        o = [mparts[:, a % 2, 0, :, part] for part in range(2)]
                    step(dve.tensor_scalar(o[0], m, -1.0, None, ALU.mult))
                    dve.scalar_tensor_tensor(out=o[1], in0=m, scalar=-1.0, in1=o[0], op0=ALU.mult, op1=ALU.subtract)\
                       .then_inc(max_parts, 1)
                elif kind == "ctxsum":
                    b = e[1]
                    dve.wait_ge(in_ctx, 16 * (2 + b))
                    step(dve.tensor_reduce(csum[:, :], ctx_sb[0:XC, :, :], AX, ALU.add))
                    if b:
                        dve.wait_ge(bank_full, nth[("mean", 0)] + 1)
                    dve.tensor_scalar(csum_r[:, :, :], csum[:, :].unsqueeze(2).broadcast_to([XC, 2, P]), 1.0 / S2,
                                      None, ALU.mult).then_inc(csum_ready, 1)
                elif kind == "fk":
                    wait_emptied(dve, e)
                    act_ = xT_sb[:, e[1], e[2], :]
                    dve.tensor_tensor(act_, act_, act_, ALU.mult).then_inc(squared, 1)
                elif kind in ("proj", "val", "norm", "wo", "fv"):
                    dve.wait_ge(bank_full, nth[e] + 1)
                    bk_ = bank(e)
                    if kind == "proj":
                        _, w, b, dc, half = e
                        k = split_no[e]
                        if k >= 2:
                            wait_split(dve, splits[k - 2])
                        v, pt = q32[:, k % 2, :], parts[:, k % 2, :, :]
                        if w == "q":
                            ins = dve.tensor_scalar(v, bk_, bq_c[:, dc:dc + 1], QSCALE, ALU.add, ALU.mult)
                        elif w == "k":
                            ins = dve.tensor_scalar(v, bk_, bk_c[:, dc:dc + 1], None, ALU.add)
                        else:
                            ins = dve.tensor_scalar(v, bk_, QSCALE if w == "c" else 1.0, None, ALU.mult)
                        ins.then_inc(dve_emptied, 1)
                        if fast(e):
                            dve.wait_ge(dve_emptied, rank[e])
                            if k >= 2:
                                wait_written(dve, k - 2)
                            step(dve.tensor_copy(pt[:, 0, :], v))
                            step(dve.tensor_tensor(v, v, pt[:, 0, :], ALU.subtract))
                            step(dve.tensor_copy(pt[:, 1, :], v))
                            dve.tensor_tensor(pt[:, 2, :], v, pt[:, 1, :], ALU.subtract).then_inc(dve_split, 1)
                    elif kind == "val":
                        _, b, half = e
                        dve.wait_ge(in_v, 16 * 3)
                        for j in range(2):
                            ins = dve.tensor_tensor(vs[:, b, 2 * half + j, :, 0:HD],
                                                    bk_[:, j * D:j * D + D].rearrange("p (h d) -> p h d", h=H),
                                                    bv_r[:, :].rearrange("p (h d) -> p h d", h=H), ALU.add)
                        ins.then_inc(dve_emptied, 1)
                    elif kind == "norm":
                        u = e[1]
                        tiles = QT if u < SELF_U else 1
                        b, g = u % SELF_U // UNITS, u % UNITS
                        turned = bk_.rearrange("p (q j c) -> p q j c", q=QT, j=HG)
                        if u:
                            wait_emptied(dve, ("norm", u - 1))
                        step(dve.reciprocal(rden[:, 0:tiles, :], turned[:, 0:tiles, :, HD]))
                        for q in range(tiles):
                            dst = attn[:, b, q, :] if u < SELF_U else tile_att[:, b, :]
                            ins = dve.tensor_tensor(
                                dst[:, 64 * g:64 * g + 64].rearrange("p (j d) -> p j d", j=HG),
                                turned[:, q, :, 0:HD], rden[:, q, :].unsqueeze(2).broadcast_to([P, HG, HD]), ALU.mult)
                        ins.then_inc(dve_emptied, 1)
                    elif kind == "wo":
                        _, b, half = e
                        dve.wait_ge(residual, b + 1)
                        r = x_sb[:, b, 2 * half:2 * half + 2, :].rearrange("p q d -> p (q d)")
                        dve.tensor_tensor(r, bk_, r, ALU.add).then_inc(dve_emptied, 1)
                    else:
                        _, b, half = e
                        wait_emptied(dve, ("fr", b, half))
                        sl = attn[:, b, 2 * half:2 * half + 2, :].rearrange("p q d -> p (q d)")
                        dve.scalar_tensor_tensor(out=sl, in0=sl, scalar=1.0, in1=bk_, op0=ALU.add, op1=ALU.mult)\
                           .then_inc(dve_emptied, 1)
                        wait_emptied(dve, e)
                        r = x_sb[:, b, 2 * half:2 * half + 2, :].rearrange("p q d -> p (q d)")
                        step(dve.scalar_tensor_tensor(out=r, in0=sl, scalar=0.5, in1=r, op0=ALU.mult, op1=ALU.add))
                elif kind == "lnA":
                    _, which, b = e
                    n = ln_no[e[1:]]
                    if which == 1:
                        wait_emptied(dve, ("wo", b, 1))
                    if which == 2:
                        dve.wait_ge(filled, b + 1)
                        step(dve.tensor_tensor(x_sb[:, b, :, :], x_sb[:, b, :, :], attn[:, b, :, :], ALU.add))
                    if n > 1:
                        dve.wait_ge(ln_done, n - 1)
                    for q in range(QT):
                        ins = dve.bn_stats(stats[:, q, :], x_sb[:, b, q, :])
                    step(ins)
                    for q in range(QT):
                        ins = dve.bn_aggr(mv[:, q, :], stats[:, q, :])
                    step(ins)
                    dve.tensor_scalar(ve[:, :], mv[:, :, 1], EPS, None, ALU.add).then_inc(var_ready, 1)
                elif kind == "lnB":
                    _, which, b = e
                    n = ln_no[e[1:]]
                    dve.wait_ge(rstd_ready, n)
                    for q in range(QT):
                        ins = dve.tensor_scalar(x_sb[:, b, q, :], x_sb[:, b, q, :], mv[:, q, 0:1], rstd[:, q:q + 1],
                                                ALU.subtract, ALU.mult)
                    ins.then_inc(ln_done, 1)
                elif kind == "select":
                    b = e[1]
                    dve.wait_ge(filled, b + 1)
                    wait_emptied(dve, ("norm", SELF_U + UNITS * b + UNITS - 1))
                    step(dve.copy_predicated(attn[:, b, LAST, :], mask_q[:, b, LAST:QT].broadcast_to([P, D]),
                                             tile_att[:, b, :]))
                elif kind == "mixB":
                    b = e[1]
                    wait_emptied(dve, ("x2T", b, CC - 1))
                    for m, (mu, mixed) in enumerate(((muk_c, xk), (mur_c, xr))):
                        for cc in range(CC):
                            dve.wait_ge(mix_prev, 4 * b + 2 * m + cc + 1)
                            dve.scalar_tensor_tensor(out=mixed[:, b, cc, :], in0=x2T[:, b, cc, 1:S + 1],
                                                     scalar=mu[:, cc:cc + 1], in1=mixed[:, b, cc, :],
                                                     op0=ALU.mult, op1=ALU.add).then_inc(mix_done, 1)
                elif kind == "rare":
                    b = e[1]

                    def settle():
                        done = order[:at_e]

                        def count(k):
                            return sum(1 for f in done if f[0] == k)
                        for s, n in ((a_max, count("A")), (exp_done, count("B")), (max_rows, count("M")),
                                     (outT_ready, count("O")), (c_done, count("O")), (filled, b + 1),
                                     (act_emptied, sum(1 for f in done if f[0] in ON_ACT)),
                                     (dve_emptied, sum(1 for f in done if f in nth and f[0] not in ON_ACT))):
                            dve.wait_ge(s, n)
                        dve.memset(gate_pad[:, :], 0.0).then_inc(gate[b], 1)

                    for t, at in rare_tiles(dve, b, settle):
                        for f in job:
                            if f[0] == "A":
                                _, g, i = f
                                if i == 0 and g >= 1:
                                    dve.wait_ge(X[b]["max2"], at("max2", g))
                                dve.wait_ge(X[b]["a_full"], at("a_full", 8 * g + i + 1))
                                dve.tensor_reduce(xm[:, i // 2, i % 2:i % 2 + 1], psA[:, i % 2, :], AX, ALU.max)\
                                   .then_inc(X[b]["a_max"], 1)
                                if i == 7:
                                    dve.wait_ge(X[b]["a_max"], at("a_max", 8 * (g + 1)))
                                    if g >= 1:
                                        dve.wait_ge(X[b]["parts"], at("parts", 3 * g))
                                    dve.tensor_reduce(xmax[:, :], xm[:, :, :], AX, ALU.max).then_inc(X[b]["max2"], 1)
                            elif f[0] == "norm":
                                g = f[1]
                                dve.wait_ge(X[b]["n_full"], at("n_full", g + 1))
                                turned = psN[:, g % 2, 0:P].rearrange("p (j c) -> p j c", j=HG)
                                if g:
                                    dve.wait_ge(X[b]["n_done"], at("n_done", 2 * g))
                                dve.reciprocal(xrd[:, :], turned[:, :, HD]).then_inc(X[b]["n_done"], 1)
                                dve.wait_ge(X[b]["n_done"], at("n_done", 2 * g + 1))
                                dve.tensor_tensor(tile_rare[:, 64 * g:64 * g + 64].rearrange("p (j d) -> p j d", j=HG),
                                                  turned[:, :, 0:HD], xrd[:, :].unsqueeze(2).broadcast_to([P, HG, HD]),
                                                  ALU.mult).then_inc(X[b]["n_done"], 1)
                        dve.wait_ge(X[b]["n_done"], at("n_done", 2 * UNITS))
                        dve.memset(gate_pad[:, :], 0.0)
                        dve.tensor_copy(mcur[:, :], mask_q[:, b, bass.ts(t, 1)]).then_inc(X[b]["n_done"], 1)
                        dve.tensor_copy(tile_sel, meanv[:, b, :]).then_inc(X[b]["n_done"], 1)
                        dve.wait_ge(X[b]["n_done"], at("n_done", 2 * UNITS + 2))
                        dve.memset(gate_pad[:, :], 0.0)
                        dve.copy_predicated(tile_sel, mcur[:, :].broadcast_to([P, D]), tile_rare)\
                           .then_inc(X[b]["n_done"], 1)
                        dve.wait_ge(X[b]["n_done"], at("n_done", 2 * UNITS + 3))
                        dve.tensor_copy(attn[:, b, bass.ts(t, 1), :].rearrange("p a d -> p (a d)"), tile_sel)\
                           .then_inc(gate[b], 1)
                    if b == 0:
                        dve.wait_ge(b_full, 8 * (SELF_A + UNITS))
                        dve.memset(x2T[:, :, :, 0:1], 0.0).then_inc(pad_ready, 1)

        @block.tensor
        def _(pe):
            def project(e, terms):
                bk_ = bank(e)
                for c0, c1, pairs in terms:
                    for n, (l, r) in enumerate(pairs):
                        ins = pe.matmul(bk_[:, c0:c1], l, r, start=(n == 0), stop=(n == len(pairs) - 1))
                ins.then_inc(bank_full, 1)

            def by_tile(e, source, w):
                half = e[2]
                project(e, [(j * D, j * D + D, [(source(c, slice((2 * half + j) * P, (2 * half + j + 1) * P)), w[:, c, :])
                                                for c in range(CC)]) for j in range(2)])

            def turn(e, sources):
                bk_ = bank(e)
                for q, src in enumerate(sources):
                    ins = pe.transpose(bk_[:, q * P:q * P + P], src, identf[:, :])
                ins.then_inc(bank_full, 1)

            for e in order:
                kind = e[0]
                if e in nth and nth[e] >= 2:
                    wait_emptied(pe, items[nth[e] - 2])
                if kind == "proj":
                    _, w, b, dc, half = e
                    if w == "x":
                        pe.wait_ge(in_ctx, 16 * (2 + b))
                        project(e, [(0, S, [(w_kv[:, c, dc * P:dc * P + P], ctx_sb[0:XC, c, half * S:half * S + S])
                                            for c in range(2)])])
                        continue
                    if w == "c":
                        pe.wait_ge(in_late, 16 * 5)
                        wait_emptied(pe, ("x1T", b, CC - 1))
                        wt = w_xq[:, :, :]
                    else:
                        pe.wait_ge(in_qk, 16 * 3)
                        if b:
                            pe.wait_ge(in_v, 16 * 3)
                        wt = w_qk[:, :, 0:D] if w == "q" else w_qk[:, :, D:2 * D]
                    project(e, [(0, S, [(wt[:, c, dc * P:dc * P + P], xT_sb[:, b, c, :]) for c in range(CC)])])
                elif kind == "val":
                    pe.wait_ge(in_v, 16 * 3)
                    by_tile(e, lambda c, t: xT_sb[:, e[1], c, t], w_v)
                elif kind == "xval":
                    _, b, i = e
                    pe.wait_ge(in_ctx, 16 * (2 + b))
                    project(e, [(j * D, j * D + D, [(ctx_sb[0:XC, c, (2 * i + j) * P:(2 * i + j + 1) * P],
                                                     w_kv[:, c, D:2 * D]) for c in range(2)]) for j in range(2)])
                elif kind == "mean":
                    pe.wait_ge(csum_ready, e[1] + 1)
                    project(e, [(0, D, [(csum_r[:, c, :], w_kv[:, c, D:2 * D]) for c in range(2)])])
                elif kind == "norm":
                    u = e[1]
                    pe.wait_ge(outT_ready, u + 1)
                    turn(e, [outT[:, q * P:q * P + P] for q in range(QT if u < SELF_U else 1)])
                elif kind == "attnT":
                    _, b, dc = e
                    wait_emptied(pe, ("norm", UNITS * b + UNITS - 1))
                    turn(e, [attn[:, b, q, dc * P:dc * P + P] for q in range(QT)])
                elif kind == "wo":
                    pe.wait_ge(in_late, 16 * 5)
                    wait_emptied(pe, ("attnT", e[1], CC - 1))
                    by_tile(e, lambda c, t: xT_sb[:, e[1], c, t], w_o)
                elif kind in ("x1T", "x2T"):
                    _, b, dc = e
                    pe.wait_ge(ln_done, ln_no[(1 if kind == "x1T" else 2, b)])
                    turn(e, [x_sb[:, b, q, dc * P:dc * P + P] for q in range(QT)])
                elif kind == "fk":
                    _, b, dc = e
                    pe.wait_ge(in_ffn, 16 * 3)
                    pe.wait_ge(mix_done, 4 * b + 2)
                    project(e, [(0, S, [(w_k2[:, c, dc * P:dc * P + P], xk[:, b, c, :]) for c in range(CC)])])
                elif kind == "fr":
                    pe.wait_ge(mix_done, 4 * e[1] + 4)
                    by_tile(e, lambda c, t: xr[:, e[1], c, t], w_r)
                elif kind == "fv":
                    pe.wait_ge(squared, CC * (e[1] + 1))
                    by_tile(e, lambda c, t: xT_sb[:, e[1], c, t], w_v2)
                elif kind == "A":
                    _, a, i = e
                    n = 8 * a + i
                    if n >= 2:
                        pe.wait_ge(a_max, n - 1)
                    if a < SELF_A:
                        b, h, q = a // PAIRS, 2 * (a % PAIRS) + i // 4, i % 4
                        if i == 0 and a % 4 == 0:
                            pe.wait_ge(rows_in[b][(a % PAIRS) // 4], 16 * 2)
                            pe.wait_ge(in_const[b], 16 * 2)
                        rows, keys = ops[b][0:SELF_ROWS, 0, h, q * P:q * P + P], ops[b][0:SELF_ROWS, 1, h, :]
                    else:
                        b, g = cross(a)
                        h, half = HG * g + i // 2, i % 2
                        if i == 0 and g == 0:
                            pe.wait_ge(kx_in[b], 16 * 2 * CC)
                            pe.wait_ge(qx_in[b], 16 * CC)
                        rows, keys = qx[b][0:SPLIT_ROWS, h, :], kx[b][0:SPLIT_ROWS, h, half * S:half * S + S]
                    pe.matmul(psA[:, n % 2, :], rows, keys, start=True, stop=True).then_inc(a_full, 1)
                elif kind == "M":
                    a = e[1]
                    pe.wait_ge(init_done, INIT)
                    pe.wait_ge(max_parts, a + 1)
                    if a >= 2:
                        pe.wait_ge(max_rows, a - 1)
                    for q in range(QT if a < SELF_A else 1):
                        ins = pe.transpose(psT[0:MAX_ROWS, a % 2, q * P:q * P + P],
                                           mparts[:, a % 2, q, :, :].rearrange("p j c -> p (j c)"), identb[:, :])
                    ins.then_inc(max_turned, 1)
                elif kind == "B":
                    _, a, i = e
                    n = 8 * a + i
                    if i == 0:
                        pe.wait_ge(max_rows, a + 1)
                    if n >= 2:
                        pe.wait_ge(exp_done, n - 1)
                    if a < SELF_A:
                        b, h, kb = a // PAIRS, 2 * (a % PAIRS) + i // 4, i % 4
                        ins = pe.matmul(psB[:, n % 2, :], ops[b][0:SELF_ROWS, 1, h, kb * P:kb * P + P],
                                        ops[b][0:SELF_ROWS, 0, h, :], start=True, stop=True)
                    else:
                        b, g = cross(a)
                        h = HG * g + i // 2
                        for k in range(4):
                            kb = 4 * (i % 2) + k
                            ins = pe.matmul(psB[:, n % 2, k * P:k * P + P], kx[b][0:CROSS_ROWS, h, kb * P:kb * P + P],
                                            qx[b][0:CROSS_ROWS, h, :], start=True, stop=True)
                    ins.then_inc(b_full, 1)
                elif kind == "C":
                    _, u, kb = e
                    b, g = u % SELF_U // UNITS, u % UNITS
                    if kb == 0:
                        pe.wait_ge(exp_done, 16 * (u + 1) if u < SELF_U else 8 * (u - SELF_U + SELF_A + 1))
                        pe.wait_ge(init_done, INIT)
                        if u:
                            pe.wait_ge(outT_ready, u)
                        if g == 0:
                            wait_emptied(pe, ("val", b, 1) if u < SELF_U else ("xval", b, XKB // 2 - 1))
                    blocks = KB if u < SELF_U else XKB
                    for j in range(HG):
                        if u < SELF_U:
                            vals, exps, w = vs[:, b, kb, HG * g + j, :], pself[:, (HG * u + j) % PRING, kb, :], S
                        else:
                            vals, exps, w = v_cross[:, b, kb, HG * g + j, :], pcross[:, (u + 1) % 2, j, kb, :], P
                        ins = pe.matmul(psC[32 * j:32 * j + VW, 0:w], vals, exps, start=(kb == 0),
                                        stop=(kb == blocks - 1))
                    if kb == blocks - 1:
                        ins.then_inc(c_done, 1)
                elif kind == "rare":
                    b = e[1]
                    for t, at in rare_tiles(pe, b):
                        for f in job:
                            if f[0] == "A":
                                _, g, i = f
                                if g == 0 and i == 0:
                                    pe.wait_ge(qx_in[b], at("qx", 16 * 2 * CC))
                                if 8 * g + i >= 2:
                                    pe.wait_ge(X[b]["a_max"], at("a_max", 8 * g + i - 1))
                                h = HG * g + i // 2
                                pe.matmul(psA[:, i % 2, :], qx[b][0:SPLIT_ROWS, h, :],
                                          kx[b][0:SPLIT_ROWS, h, (i % 2) * S:(i % 2) * S + S], start=True, stop=True)\
                                  .then_inc(X[b]["a_full"], 1)
                            elif f[0] == "M":
                                g = f[1]
                                pe.wait_ge(X[b]["parts"], at("parts", 3 * (g + 1)))
                                if g:
                                    pe.wait_ge(X[b]["rows"], at("rows", g))
                                pe.transpose(psT[0:MAX_ROWS, 0, 0:P], xparts[:, :, :].rearrange("p j c -> p (j c)"),
                                             identb[:, :]).then_inc(X[b]["turned"], 1)
                            elif f[0] == "B":
                                _, g, i = f
                                if i == 0:
                                    pe.wait_ge(X[b]["rows"], at("rows", g + 1))
                                if 8 * g + i >= 2:
                                    pe.wait_ge(X[b]["exp"], at("exp", 8 * g + i - 1))
                                h = HG * g + i // 2
                                for k in range(4):
                                    kb = 4 * (i % 2) + k
                                    ins = pe.matmul(psB[:, i % 2, k * P:k * P + P],
                                                    kx[b][0:CROSS_ROWS, h, kb * P:kb * P + P],
                                                    qx[b][0:CROSS_ROWS, h, :], start=True, stop=True)
                                ins.then_inc(X[b]["b_full"], 1)
                            elif f[0] == "C":
                                _, g, kb = f
                                if kb == 0:
                                    pe.wait_ge(X[b]["exp"], at("exp", 8 * (g + 1)))
                                    if g:
                                        pe.wait_ge(X[b]["outT"], at("outT", g))
                                for j in range(HG):
                                    ins = pe.matmul(psC[32 * j:32 * j + VW, 0:P], v_cross[:, b, kb, HG * g + j, :],
                                                    pcross[:, RARE, j, kb, :], start=(kb == 0), stop=(kb == XKB - 1))
                                if kb == XKB - 1:
                                    ins.then_inc(X[b]["c_done"], 1)
                            elif f[0] == "norm":
                                g = f[1]
                                pe.wait_ge(X[b]["outT"], at("outT", g + 1))
                                if g >= 2:
                                    pe.wait_ge(X[b]["n_done"], at("n_done", 2 * (g - 1)))
                                pe.transpose(psN[:, g % 2, 0:P], outT[:, 0:P], identf[:, :])\
                                  .then_inc(X[b]["n_full"], 1)


def kernel(**inputs):
    import ml_dtypes
    import numpy as np
    import concourse.bacc as bacc
    from concourse.bass_utils import run_bass_kernel_spmd as run

    def arr(name):
        return np.asarray(inputs[name])

    def by_head(b):
        return np.ascontiguousarray(b.reshape(CC, H // CC, HD).transpose(2, 1, 0).reshape(P, CC))

    def columns(w):
        return np.ascontiguousarray(w.reshape(-1, CC, H // CC, HD).transpose(0, 1, 3, 2).reshape(-1, D))

    def T(a):
        return np.ascontiguousarray(np.swapaxes(a, -1, -2))

    slopes = (np.float32(1) / np.float32(2) ** (np.arange(H, dtype=np.float32) / np.float32(H))).astype(np.float32)
    term = slopes[:, None] * np.arange(S, dtype=np.float32)[None, :]
    hi = term.astype(ml_dtypes.bfloat16)
    mid = (term - hi.astype(np.float32)).astype(ml_dtypes.bfloat16)
    low = (term - hi.astype(np.float32) - mid.astype(np.float32)).astype(ml_dtypes.bfloat16)
    one = np.ones_like(hi)
    mine = [one * (np.arange(H) % HG == r // 2).astype(ml_dtypes.bfloat16)[:, None] for r in range(MAX_ROWS)]
    k_rows = np.stack(mine + [hi, mid, low])
    q_rows = np.stack([0 * one] * MAX_ROWS + [one, one, one])
    kvT = T(arr("L0_xattn_Wkv"))
    data = {
        "x": arr("x"), "xT": T(arr("x")), "ctxT": T(arr("ctx_768")), "mask": arr("mask_BxS_bk0"),
        "w_qk": np.concatenate([columns(arr("L0_attn_Wq")), columns(arr("L0_attn_Wk"))], axis=1),
        "cols": np.concatenate([by_head(arr("L0_attn_bq")), by_head(arr("L0_attn_bk")), T(arr("L0_ffn_mu_r").reshape(CC, P)),
                                T(arr("L0_ffn_mu_k").reshape(CC, P))], axis=1), "wv": arr("L0_attn_Wv"), "bv": arr("L0_attn_bv"), "wo": arr("L0_attn_Wo"),
        "bo": arr("L0_attn_bo"), "xwqT": columns(T(arr("L0_xattn_Wq"))), "xwkvT": np.concatenate([columns(kvT[:, :D]), kvT[:, D:]], axis=1),
        "wrT": T(arr("L0_ffn_W_r")), "wkT": T(arr("L0_ffn_W_k")), "wvT": T(arr("L0_ffn_W_v")),
        "k_rows": k_rows, "q_rows": q_rows, "ident": np.eye(P, dtype=np.float32),
    }
    nc = bacc.Bacc("TRN2", target_bir_lowering=False, num_devices=1)
    arrays, args = {}, []
    for name, a in data.items():
        a = np.ascontiguousarray(a)
        arrays[f"in_{name}"] = a
        args.append(nc.dram_tensor(f"in_{name}", a.shape, mybir.dt.from_np(a.dtype), kind="ExternalInput").ap())
    args.append(nc.dram_tensor("out_x", (B, S, D), F32, kind="ExternalOutput").ap())
    decoder_layer(nc, *args)
    return run(nc, [arrays], core_ids=[0]).results[0]["out_x"]
```

```python
from contextlib import ExitStack

import concourse.bass as bass
from concourse import mybir

F32 = mybir.dt.float32
BF16 = mybir.dt.bfloat16
I32 = mybir.dt.int32
U8 = mybir.dt.uint8
ALU = mybir.AluOpType
ACT = mybir.ActivationFunctionType
AX = mybir.AxisListType.X

P = 128
B, S, D = 2, 512, 256
H, HD = 16, 16
S2, DC = 1024, 192
CC = D // P
XC = 96
QT = S // P
KB = S // P
XKB = S2 // P
HG = 4
UNITS = H // HG
PAIRS = H // 2
VW = HD + 1
EPS = 1e-5
QSCALE = float(HD) ** -0.5
Q_PARTS = (0, 0, 0, 1, 1, 2)
K_PARTS = (2, 0, 1, 0, 1, 0)
SPLIT_ROWS = HD * len(Q_PARTS)
MAX_ROW = SPLIT_ROWS
MAX_ROWS = 2 * HG
CROSS_ROWS = SPLIT_ROWS + MAX_ROWS
SELF_ROWS = CROSS_ROWS + 3
PRING = 6


SELF_A = B * PAIRS
CROSS_A = B * UNITS
SELF_U = B * UNITS
LAST = QT - 1
GAP = 1
WARM_UP = 11
SELF_C_AT = (1, 2, 5, 6)
NORM_AT = 0
CROSS_C_AT = (0, 1, 2, 2, 3, 3, 4, 4)
CROSS_NORM_AT = 5
M_AT = 3


PARTS = ((0, LAST), (LAST, QT))


def by_bank(part):
    lo, hi = PARTS[part]
    return [(q, min(q + 2, hi)) for q in range(lo, hi, 2)]


def plan():
    at_step = list(range(SELF_A + UNITS)) + [None] * GAP + list(range(SELF_A + UNITS, SELF_A + CROSS_A))
    when = {a: s for s, a in enumerate(at_step) if a is not None}
    last_step = max(when.values()) + 3

    def two(kind, b):
        return [(kind, b, n) for n in range(2)]

    def x2T(b, part):
        return [("x2T", b, part, cc) for cc in range(CC)]

    def fk(b, part):
        return [("fk", b, part, dc) for dc in range(CC)]

    def fr(b, part):
        return [("fr", b, part, n) for n in range(len(by_bank(part)))]

    def fv(b, part):
        return [("fv",) + e[1:] for e in fr(b, part)]

    order = [("proj", "q", 0, 0, 0), ("proj", "k", 0, 0, 0), ("proj", "q", 0, 1, 0)] + two("val", 0)
    order += [("xval", 0, n) for n in range(XKB // 2)]
    placed = {
        0: {2: [("proj", "k", 0, 1, 0)]},
        1: {1: [("proj", "q", 1, 0, 0)], 7: [("bias", 0), ("proj", "x", 0, 0, 0)]},
        2: {0: [("bias", 1)]},
        3: {5: [("proj", "k", 1, 0, 0)]},
        5: {0: [("proj", "x", 0, 0, 1)], 1: [("val", 1, 0)], 4: [("proj", "x", 0, 1, 0)],
            5: [("proj", "x", 0, 1, 1)]},
        6: {4: [("ctxsum", 0)], 7: [("mean", 0)]},
        7: {1: [("proj", "q", 1, 1, 0)], 4: [("val", 1, 1)], 5: [("ctxload", 1)]},
        9: {5: [("proj", "k", 1, 1, 0)], 7: [("proj", "x", 1, 0, 0)]},
        10: {3: [("ctxsum", 1)]},
        11: {1: [("xval", 1, 0), ("attnT", 0, 0), ("attnT", 0, 1)], 5: [("wo", 0, 1)],
             7: [("lnA", 1, 0, 1), ("proj", "x", 1, 0, 1)]},
        12: {2: [("wo", 0, 0), ("lnB", 1, 0, 1)], 4: [("lnA", 1, 0, 0)]},
        13: {4: [("x1T", 0)], 7: [("proj", "c", 0, 0, 0), ("lnB", 1, 0, 0), ("qxread", 0)]},
        14: {2: [("proj", "x", 1, 1, 0)]},
        15: {5: [("proj", "x", 1, 1, 1)], 7: [("xval", 1, 1)]},
        16: {2: [("fill", 0), ("xval", 1, 2)]},
        17: {7: [("mean", 1)]},
        18: {7: [("xval", 1, 3)]},
        19: {0: [("rare", 0)], 1: [("attnT", 1, 0), ("attnT", 1, 1)], 3: [("wo", 1, 1), ("lnA", 1, 1, 1)],
             5: [("lnB", 1, 1, 1)], 7: [("x1T", 1)]},
        20: {0: [("proj", "c", 1, 0, 0), ("wo", 1, 0), ("lnA", 1, 1, 0)], 1: [("sum", 0)], 2: [("lnB", 1, 1, 0)],
             3: [("qxread", 1)], 5: [("lnA", 2, 0, 0)], 6: [("lnB", 2, 0, 0)]},
        21: {2: [("x2T", 0, 0, 0), ("x2T", 0, 0, 1), ("mixA", 0, 0)], 4: [("mixB", 0, 0)], 6: [("fk", 0, 0, 0)],
             7: [("fill", 1), ("rare", 1), ("sum", 1)]},
        22: {0: [("fk", 0, 0, 1)], 1: [("fr", 0, 0, 0)], 2: [("lnA", 2, 1, 0), ("fr", 0, 0, 1)],
             4: [("lnB", 2, 1, 0)], 5: [("fv", 0, 0, 1)],
             6: [("x2T", 1, 0, 0), ("select", 0), ("x2T", 1, 0, 1), ("lnA", 2, 0, 1), ("mixA", 1, 0),
                 ("mixB", 1, 0)]},
        23: {0: [("fv", 0, 0, 0)], 1: [("lnB", 2, 0, 1)], 3: [("fk", 1, 0, 0)], 4: [("x2T", 0, 1, 0)],
             5: [("x2T", 0, 1, 1)], 6: [("mixA", 0, 1), ("fk", 1, 0, 1)],
             7: [("fr", 1, 0, 0), ("fr", 1, 0, 1), ("mixB", 0, 1), ("fv", 1, 0, 1)]},
        24: {0: [("fr", 0, 1, 0)], 5: [("lnA", 3, 0, 0)], 6: [("lnB", 3, 0, 0)], 7: [("fk", 0, 1, 0)]},
        25: {2: [("fk", 0, 1, 1), ("fv", 1, 0, 0)], 3: [("lnA", 3, 1, 0)], 7: [("fv", 0, 1, 0)]},
        26: {0: [("lnB", 3, 1, 0)], 1: [("lnA", 3, 0, 1)], 6: [("lnB", 3, 0, 1)]},
    }
    for s in range(last_step + 1):
        m = next((a for a in when if when[a] == s - 1), None)
        if m is not None:
            order.append(("chain", m))
        for i in range(8):
            if s < len(at_step) and at_step[s] is not None:
                order.append(("A", at_step[s], i))
            a = next((a for a in when if when[a] == s - 2), None)
            if a is not None:
                order.append(("B", a, i))
            if i == M_AT and m is not None:
                order.append(("M", m))
            u, odd = (s - 4) // 2, (s - 4) % 2
            if 0 <= u < SELF_U and odd and i == NORM_AT:
                order.append(("norm", u))
            order += placed.get(s, {}).get(i, [])
            if 0 <= u < SELF_U and not odd and i in SELF_C_AT:
                order.append(("C", u, SELF_C_AT.index(i)))
                if i == SELF_C_AT[-1]:
                    order.append(("O", u))
            c = next((a for a in when if when[a] == s - 3 and a >= SELF_A), None)
            if c is not None:
                u = SELF_U + c - SELF_A
                order += [("C", u, kb) for kb in range(XKB) if CROSS_C_AT[kb] == i]
                if i == CROSS_C_AT[-1]:
                    order.append(("O", u))
                if i == CROSS_NORM_AT:
                    order.append(("norm", u))
        if s == PAIRS + 2:
            order.append(("kxread", 0))
        if s == when[SELF_A - 1] + 2:
            order.append(("kxread", 1))
    b = B - 1
    order += [("select", b), ("lnA", 2, b, 1), ("lnB", 2, b, 1)] + x2T(b, 1) + [("mixA", b, 1), ("mixB", b, 1)]
    order += fk(b, 1) + fr(b, 1) + fv(b, 1) + [("lnA", 3, b, 1), ("lnB", 3, b, 1)]
    return order


def decoder_layer(nc, x, xT, ctxT, mask, wqk, cols, wv, bv, wo, bo, xwqT, xwkvT, wrT, wkT, wvT, k_rows, q_rows, ident,
                  out):
    order = plan()
    items = [e for e in order if e[0] in ("proj", "val", "xval", "mean", "norm", "attnT", "wo", "x1T", "x2T", "fk",
                                          "fr", "fv", "M")]
    nth = {e: n for n, e in enumerate(items)}
    ON_ACT = ("xval", "mean", "attnT", "x1T", "x2T", "fk", "fr", "M")
    rank = {}
    for e in items:
        rank[e] = sum(1 for f in items[:nth[e] + 1] if (f[0] in ON_ACT) == (e[0] in ON_ACT))
    splits = [e for e in items if e[0] == "proj"]
    split_no = {e: k for k, e in enumerate(splits)}
    mixB_no = {e: n for n, e in enumerate(e for e in order if e[0] == "mixB")}
    fk_no = {e: n + 1 for part in range(2) for n, e in enumerate(e for e in order if e[0] == "fk" and e[2] == part)}
    ln_no = {e[1:]: n + 1 for n, e in enumerate(e for e in order if e[0] == "lnA")}

    def fast(e):
        return e[1] == "c" or e in splits[:2]

    split_rank = {e: sum(1 for f in splits[:split_no[e] + 1] if fast(f) == fast(e)) for e in splits}

    ctx = ExitStack()
    with ctx:
        def sb(name, shape, dt=F32):
            return ctx.enter_context(nc.sbuf_tensor(name, shape, dt))

        def ps(name, shape, dt=F32):
            return ctx.enter_context(nc.psum_tensor(name, shape, dt))

        def sem(name):
            return ctx.enter_context(nc.semaphore(name))

        ops = [sb(f"ops{b}", [P, 2, H, S], BF16) for b in range(B)]
        kx = [ops[b][:, :, :, :].rearrange("p a h t -> p (a h t)").rearrange("p (h t) -> p h t", h=H) for b in range(B)]
        probs = sb("probs", [P, PRING * KB * S])
        pself = probs[:, :].rearrange("p (r k t) -> p r k t", r=PRING, k=KB)
        pcross = probs[:, :].rearrange("p (u j k t) -> p u j k t", u=3, j=HG, k=XKB)
        RARE = 2
        v_self = sb("v_self", [P, B * KB * H * VW])
        vs = v_self[:, :].rearrange("p (b k h d) -> p b k h d", b=B, k=KB, h=H)
        v_cross = sb("v_cross", [P, B, XKB, H, VW])
        x_sb = sb("x_sb", [P, B, QT, D])
        xT_sb = sb("xT_sb", [P, B, CC, S])
        ctx_sb = sb("ctx_sb", [P, 2, S2])
        attn = sb("attn", [P, B, QT, D])
        w_qk = sb("w_qk", [P, CC, 2 * D])
        w_v, w_o, w_xq = (sb(f"w{n}", [P, CC, D]) for n in ("v", "o", "xq"))
        w_kv = sb("w_kv", [XC, 2, 2 * D])
        qx0 = sb("qx0", [P, H * P], BF16)
        qx = [a.rearrange("p (h c t) -> p h c t", h=H // CC, c=CC)
              for a in (qx0[:, :], w_qk[:, :, :].rearrange("p c n -> p (c n)").bitcast(BF16))]
        qrare = qx[::-1]
        q32 = sb("q32", [P, 2, S])
        parts = sb("parts", [P, 2, 3, S], BF16)
        warm = parts[:, 1, 0, :]
        outT = sb("outT", [P, S])
        identf = sb("identf", [P, P])
        identb = sb("identb", [P, P], BF16)
        cols_sb = sb("cols_sb", [P, 4, CC])
        bq_c, bk_c, mur_c, muk_c = (cols_sb[:, n, :] for n in range(4))
        bv_r, bo_r = sb("bv_r", [P, D]), sb("bo_r", [P, D])
        om_r, om_k = sb("om_r", [P, CC]), sb("om_k", [P, CC])
        meanv = sb("meanv", [P, B, D])
        csum = sb("csum", [XC, 2])
        csum_r = sb("csum_r", [XC, 2, P])
        mx = sb("mx", [P, 2, 8])
        mparts = sb("mparts", [P, 2, QT, HG, 2], BF16)
        rden = sb("rden", [P, QT, HG])
        stats = sb("stats", [P, QT, 6])
        mv = sb("mv", [P, QT, 2])
        ve = sb("ve", [P, QT])
        rstd = sb("rstd", [P, QT])
        nhalf = sb("nhalf", [P, QT])
        minus = sb("minus", [P, HG])
        mask_q = sb("mask_q", [P, B, QT], U8)
        mask_row = sb("mask_row", [1, B, QT, P], U8)
        live = sb("live", [1, B, QT])
        weight = sb("weight", [1, B, QT])
        behind = sb("behind", [1, 1])
        count_i = sb("count_i", [1, 1], I32)
        xm = sb("xm", [P, HG, 2])
        xmax = sb("xmax", [P, HG])
        xres = sb("xres", [P, HG])
        xparts = sb("xparts", [P, HG, 2], BF16)
        xrd = sb("xrd", [P, HG])
        cmax = sb("cmax", [P, HG])
        tile_att, tile_rare, tile_sel = w_v, bv_r[:, :], bo_r[:, :]
        mcur = sb("mcur", [P, 1], U8)
        gate_pad = sb("gate_pad", [P, 1])
        w_r, w_k2, w_v2 = (v_self[:, n * CC * D:(n + 1) * CC * D].rearrange("p (c d) -> p c d", c=CC) for n in range(3))
        rooms = [ctx_sb[:, :, :].rearrange("p a t -> p (a t)"),
                 ops[0][:, :, :, :].rearrange("p a h t -> p (a h t)").bitcast(F32)]
        xr, xk = ([a[:, n * CC * S:(n + 1) * CC * S].rearrange("p (c t) -> p c t", c=CC) for a in rooms] for n in range(2))

        psA = ps("psA", [P, 3, S])
        psB = ps("psB", [P, 2, S])
        psC = ps("psC", [P, S])
        psN = ps("psN", [P, 2, S])
        turned_rare = psA[:, 2, :].bitcast(BF16)[0:MAX_ROWS, 0:P]

        GROUPS = len(Q_PARTS)
        scr = {w: nc.dram_tensor(f"scr_{w}", [B, CC, GROUPS, HD, H // CC, S2 if w == "x" else S], BF16).ap()
               for w in "qkx"}
        scr_tile, scr_rare = (nc.dram_tensor(name, [B, GROUPS, HD, H // CC, CC, P], BF16).ap()
                              for name in ("scr_tile", "scr_rare"))

        in_qk, in_ident, in_v, in_ctx, in_late, in_mask, in_ffn = (
            sem(n) for n in ("in_qk", "in_ident", "in_v", "in_ctx", "in_late", "in_mask", "in_ffn"))
        in_const = [sem(f"in_const{b}") for b in range(B)]
        init_done = sem("init_done")
        INIT = 7
        warm_ready = sem("warm_ready")
        bank_full = sem("bank_full")
        dve_emptied, act_emptied = sem("dve_emptied"), sem("act_emptied")
        dve_split, pool_split = sem("dve_split"), sem("pool_split")
        scr_written = [sem(f"scr_written{n}") for n in range(2)]
        rows_in = [[sem(f"rows_in{b}{dc}") for dc in range(CC)] for b in range(B)]
        kx_in = [sem(f"kx_in{b}") for b in range(B)]
        qx_in = [sem(f"qx_in{b}") for b in range(B)]
        qrare_out, qrare_in = ([sem(f"qrare_{w}{b}") for b in range(B)] for w in ("out", "in"))
        csum_ready = sem("csum_ready")
        a_full, a_max = sem("a_full"), sem("a_max")
        max_parts = sem("max_parts")
        b_full, exp_done = sem("b_full"), sem("exp_done")
        c_done, outT_ready = sem("c_done"), sem("outT_ready")
        var_ready, rstd_ready, ln_done = sem("var_ready"), sem("rstd_ready"), sem("ln_done")
        residual, filled = sem("residual"), sem("filled")
        dve_step, pool_step = sem("dve_step"), sem("pool_step")
        count_ready = sem("count_ready")
        passed = sem("passed")
        gate = [sem(f"gate{b}") for b in range(B)]
        rare_over = [sem(f"rare_over{b}") for b in range(B)]
        X = [{n: sem(f"x{n}{b}") for n in ("a_full", "a_max", "max2", "parts", "turned", "rows", "b_full", "exp", "c_done",
                                           "outT", "n_full", "n_done", "q_dve", "q_pe", "q_act")} for b in range(B)]
        XTOT = {"a_full": 32, "a_max": 32, "parts": 12, "max2": 4, "turned": 4, "rows": 4, "b_full": 32, "exp": 32,
                "c_done": 4, "outT": 4, "n_full": 4, "n_done": 11, "qx": 16, "q_out": 16 * 3, "q_dve": 6,
                "q_pe": 2, "q_act": 1}
        om_ready, first_ready, mix_prev, mix_done, summed, stored = (
            sem(n) for n in ("om_ready", "first_ready", "mix_prev", "mix_done", "summed", "stored"))

        squared = [sem(f"squared{part}") for part in range(2)]

        def bank(e):
            return psN[:, nth[e] % 2, :]

        def wait_emptied(eng, e):
            eng.wait_ge(act_emptied if e[0] in ON_ACT else dve_emptied, rank[e])

        def wait_split(eng, e):
            eng.wait_ge(dve_split if fast(e) else pool_split, split_rank[e])

        def square(eng, e):
            _, b, part, dc = e
            lo, hi = PARTS[part]
            wait_emptied(eng, e)
            k_act = xT_sb[:, b, dc, lo * P:hi * P]
            eng.tensor_tensor(k_act, k_act, k_act, ALU.mult).then_inc(squared[part], 1)

        def groups(w, j):
            if w in "qc":
                return (slice(0, 3), slice(3, 5), slice(5, 6))[j]
            return (slice(1, 6, 2), slice(2, 5, 2), slice(0, 1))[j]

        def width(w):
            return CC * P if w == "c" else S

        def wait_written(eng, k):
            eng.wait_ge(scr_written[k % 2], 16 * 3 * (k // 2 + 1))

        def cross(a):
            return (a - SELF_A) // UNITS, (a - SELF_A) % UNITS

        job = []
        for s in range(UNITS + 2):
            for i in range(8):
                if s < UNITS:
                    job.append(("A", s, i))
                if i < 4 and s >= 2:
                    job += [("C", s - 2, 2 * i), ("C", s - 2, 2 * i + 1)]
                if i == 3:
                    if s >= 2:
                        job += [("O", s - 2), ("norm", s - 2)]
                    if 1 <= s <= UNITS:
                        job.append(("M", s - 1))
                if i >= 4 and 1 <= s <= UNITS:
                    job.append(("B", s - 1, i - 4))
            if 1 <= s <= UNITS:
                job += [("B", s - 1, i) for i in range(4, 8)]

        def of_group(q_rows_, g):
            h = HG * g % (H // CC)
            return q_rows_[MAX_ROW:CROSS_ROWS, h:h + HG, HG * g // (H // CC), :]

        def of_head(q_rows_, rows, h):
            return q_rows_[0:rows, h % (H // CC), h // (H // CC), :]

        counts = {}

        def load_count(eng):
            eng.wait_ge(count_ready, 1)
            counts[eng] = eng.value_load(count_i[0:1, 0:1], min_val=0, max_val=QT - 1)

        def rare_tiles(eng, b, ahead=lambda: None):
            count = counts[eng]
            with eng.If(count > 0):
                ahead()
                with eng.Fori(0, count) as n:
                    def at(name, c):
                        return n * XTOT[name] + c
                    eng.wait_ge(gate[b], n + 1)
                    eng.sem_inc(passed, 1)
                    yield (LAST - 1) - n, at
                if eng is nc.vector:
                    eng.memset(gate_pad[:, :], 0.0).then_inc(rare_over[b], 1)
                eng.wait_ge(rare_over[b], 1)

        block = ctx.enter_context(nc.Block())

        @block.sync
        def _(sp):
            def load(dst, src, s):
                sp.dma_start(dst, src).then_inc(s, 16)

            def wide(w):
                return w.rearrange("(c p) n -> p c n", p=P)

            def stacked(w, b, dc):
                return scr[w][b, dc].rearrange("g d h t -> (g d) h t")

            load(xT_sb[:, 0, :, :], xT[0].rearrange("(c p) t -> p c t", p=P), in_qk)
            load(w_qk[:, :, :], wide(wqk), in_qk)
            load(cols_sb[:, :, :].rearrange("p n c -> p (n c)"), cols, in_qk)
            load(w_v[:, :, :], wide(wv), in_v)
            load(bv_r[:, :], bv.rearrange("(a n) -> a n", a=1).broadcast_to([P, D]), in_v)
            load(xT_sb[:, 1, :, :], xT[1].rearrange("(c p) t -> p c t", p=P), in_v)
            load(ctx_sb[0:XC, :, :], ctxT[0].rearrange("(c p) t -> p c t", p=XC), in_ctx)
            load(w_kv[:, :, :], xwkvT.rearrange("(c p) n -> p c n", p=XC), in_ctx)
            for e in order:
                if e == ("A", 0, 0):
                    load_count(sp)
                elif e[0] == "proj":
                    _, w, b, dc, half = e
                    k = split_no[e]
                    cut = slice(half * S, half * S + S)
                    wait_split(sp, e)
                    if w == "c":
                        places = scr_tile[b].rearrange("g d h c t -> (d h) g (c t)")
                    else:
                        places = scr[w][b, dc].rearrange("g d h t -> (d h) g t")[:, :, cut]
                    for j in range(3):
                        dst = places[:, groups(w, j), :]
                        sp.dma_start(dst, parts[:, k % 2, j, 0:width(w)].unsqueeze(1).broadcast_to(list(dst.shape)))\
                          .then_inc(scr_written[k % 2], 16)
                    if w == "k":
                        for op, split in ((0, split_no[("proj", "q") + e[2:]]), (1, k)):
                            wait_written(sp, split)
                            load(ops[b][0:SPLIT_ROWS, op, 8 * dc:8 * dc + 8, :], stacked("qk"[op], b, dc), rows_in[b][dc])
                elif e == ("ctxload", 1):
                    sp.wait_ge(bank_full, nth[("mean", 0)] + 1)
                    sp.wait_ge(csum_ready, 1)
                    load(ctx_sb[0:XC, :, :], ctxT[1].rearrange("(c p) t -> p c t", p=XC), in_ctx)
                elif e[0] == "kxread":
                    b = e[1]
                    last = split_no[("proj", "x", b, CC - 1, 1)]
                    wait_written(sp, last)
                    wait_written(sp, last - 1)
                    sp.wait_ge(b_full, 8 * PAIRS * (b + 1))
                    for dc in range(CC):
                        load(kx[b][0:SPLIT_ROWS, 8 * dc:8 * dc + 8, :], stacked("x", b, dc), kx_in[b])
                        load(kx[b][MAX_ROW:CROSS_ROWS, :, dc * S:dc * S + S], k_rows[0:MAX_ROWS, :, :], kx_in[b])
                elif e[0] == "qxread":
                    b = e[1]
                    wait_written(sp, split_no[("proj", "c", b, 0, 0)])
                    load(qx[b][0:SPLIT_ROWS, :, :, :], scr_tile[b].rearrange("g d h c t -> (g d) h c t"), qx_in[b])
                    if b == B - 1:
                        sp.wait_ge(c_done, SELF_U)
                        for dst, src in ((w_k2, wkT), (w_r, wrT), (w_v2, wvT)):
                            load(dst, wide(src), in_ffn)
                elif e[0] == "rare":
                    b = e[1]
                    for t, at in rare_tiles(sp, b):
                        sp.wait_ge(X[b]["q_dve"], at("q_dve", 6))
                        for j in range(3):
                            dst = scr_rare[b].rearrange("g d h c t -> (d h) g (c t)")[:, groups("c", j), :]
                            load(dst, parts[:, 0, j, 0:CC * P].unsqueeze(1).broadcast_to(list(dst.shape)), qrare_out[b])
                        sp.wait_ge(qrare_out[b], at("q_out", 16 * 3))
                        load(qrare[b][0:SPLIT_ROWS, :, :, :], scr_rare[b].rearrange("g d h c t -> (g d) h c t"),
                             qrare_in[b])
                elif e[0] == "lnB" and e[1] == 3:
                    _, _, b, part = e
                    lo, hi = PARTS[part]
                    sp.wait_ge(ln_done, ln_no[e[1:]])
                    load(out[b].rearrange("(q p) d -> p q d", p=P)[:, lo:hi, :], x_sb[:, b, lo:hi, :], stored)
            sp.wait_ge(stored, 16 * B * 2)

        @block.gpsimd
        def _(pool):
            steps = [0]

            def step(ins):
                steps[0] += 1
                ins.then_inc(pool_step, 1)
                pool.wait_ge(pool_step, steps[0])

            pool.memset(mparts[:, :, :, :, :], 0.0).then_inc(init_done, 1)
            pool.memset(vs[:, :, :, :, HD:VW], 1.0).then_inc(init_done, 1)
            pool.memset(v_cross[:, :, :, :, HD:VW], 1.0).then_inc(init_done, 1)
            pool.memset(minus[:, :], -1.0).then_inc(init_done, 1)
            pool.memset(nhalf[:, :], -0.5).then_inc(init_done, 1)
            for e in order:
                if e == ("A", 0, 0):
                    load_count(pool)
                elif e[0] == "bias":
                    b = e[1]
                    pool.wait_ge(in_late, 16 * 5)
                    for q in range(QT):
                        ins = pool.tensor_tensor(x_sb[:, b, q, :], x_sb[:, b, q, :], bo_r[:, :], ALU.add)
                    ins.then_inc(residual, 1)
                elif e[0] == "proj" and not fast(e):
                    k = split_no[e]
                    pool.wait_ge(dve_emptied, rank[e])
                    if k >= 2:
                        wait_written(pool, k - 2)
                    v, pt = q32[:, k % 2, :], parts[:, k % 2, :, :]
                    step(pool.tensor_copy(pt[:, 0, :], v))
                    step(pool.tensor_tensor(v, v, pt[:, 0, :], ALU.subtract))
                    step(pool.tensor_copy(pt[:, 1, :], v))
                    pool.tensor_tensor(pt[:, 2, :], v, pt[:, 1, :], ALU.subtract).then_inc(pool_split, 1)
                elif e[0] == "fk" and e[2] == 0:
                    square(pool, e)
                elif e[0] == "sum":
                    b = e[1]
                    lo, hi = PARTS[0]
                    pool.wait_ge(ln_done, ln_no[(1, b, 0)])
                    pool.wait_ge(filled, b + 1)
                    for q in range(lo, hi):
                        ins = pool.tensor_tensor(x_sb[:, b, q, :], x_sb[:, b, q, :], attn[:, b, q, :], ALU.add)
                    ins.then_inc(summed, 1)
                elif e[0] == "lnA":
                    pool.wait_ge(init_done, INIT)
                    lo, hi = PARTS[e[3]]
                    pool.wait_ge(var_ready, ln_no[e[1:]])
                    pool.tensor_tensor(rstd[:, lo:hi], ve[:, lo:hi], nhalf[:, lo:hi], ALU.pow).then_inc(rstd_ready, 1)
                elif e[0] == "rare":
                    b = e[1]
                    for t, at in rare_tiles(pool, b):
                        for f in job:
                            if f[0] == "M":
                                g = f[1]
                                pool.wait_ge(X[b]["max2"], at("max2", g + 1))
                                if g >= 1:
                                    pool.wait_ge(X[b]["turned"], at("turned", g))
                                pool.tensor_tensor(xparts[:, :, 0], xmax[:, :], minus[:, :], ALU.mult)\
                                    .then_inc(X[b]["parts"], 1)
                                pool.wait_ge(X[b]["parts"], at("parts", 3 * g + 1))
                                pool.tensor_tensor(xres[:, :], xmax[:, :], xparts[:, :, 0], ALU.add)\
                                    .then_inc(X[b]["parts"], 1)
                                pool.wait_ge(X[b]["parts"], at("parts", 3 * g + 2))
                                pool.tensor_tensor(xparts[:, :, 1], xres[:, :], minus[:, :], ALU.mult)\
                                    .then_inc(X[b]["parts"], 1)

        @block.scalar
        def _(act):
            act.dma_start(identf[:, :], ident).then_inc(in_ident, 16)
            act.dma_start(mask_row[0:1, :, :, :], mask.rearrange("(a b) (q p) -> a b q p", a=1, p=P))\
               .then_inc(in_mask, 16)
            act.dma_start(ops[0][MAX_ROW:SELF_ROWS, 0, :, :], q_rows).then_inc(in_const[0], 16)
            act.dma_start(ops[0][MAX_ROW:SELF_ROWS, 1, :, :], k_rows).then_inc(in_const[0], 16)
            with nc.allow_non_contiguous_dma(reason="one byte for each query"):
                act.dma_start(mask_q[:, :, :], mask.rearrange("b (q p) -> p b q", p=P)).then_inc(in_mask, 16)
            act.wait_ge(in_ident, 16)
            act.activation(identb[:, :], identf[:, :], ACT.Copy).then_inc(init_done, 1)
            for e in order:
                kind = e[0]
                if e == ("A", 0, 0):
                    act.wait_ge(rows_in[0][0], 16 * 2)
                    b = B - 1
                    act.dma_start(ops[b][MAX_ROW:SELF_ROWS, 0, :, :], q_rows).then_inc(in_const[b], 16)
                    act.dma_start(ops[b][MAX_ROW:SELF_ROWS, 1, :, :], k_rows).then_inc(in_const[b], 16)
                    act.dma_start(x_sb[:, 0, :, :], x[0].rearrange("(q p) d -> p q d", p=P)).then_inc(in_late, 16)
                    act.dma_start(x_sb[:, 1, :, :], x[1].rearrange("(q p) d -> p q d", p=P)).then_inc(in_late, 16)
                    act.dma_start(bo_r[:, :], bo.rearrange("(a n) -> a n", a=1).broadcast_to([P, D])).then_inc(in_late, 16)
                    act.dma_start(w_o[:, :, :], wo.rearrange("(c p) n -> p c n", p=P)).then_inc(in_late, 16)
                    act.dma_start(w_xq[:, :, :], xwqT.rearrange("(c p) n -> p c n", p=P)).then_inc(in_late, 16)
                    load_count(act)
                if kind == "B":
                    _, a, i = e
                    n = 8 * a + i
                    if a < SELF_A:
                        head = 2 * a + i // 4
                        if i % 4 == 0 and head >= PRING:
                            act.wait_ge(c_done, (head - PRING) // HG + 1)
                        dst = pself[:, head % PRING, i % 4, :]
                    else:
                        u = a - SELF_A + SELF_U
                        if i == 0:
                            act.wait_ge(c_done, u - 1)
                        dst = pcross[:, (u + 1) % 2, i // 2, 4 * (i % 2):4 * (i % 2) + 4, :]\
                            .rearrange("p k t -> p (k t)")
                    act.wait_ge(b_full, n + 1)
                    act.activation(dst, psB[:, n % 2, :], ACT.Exp).then_inc(exp_done, 1)
                elif kind == "M":
                    a = e[1]
                    act.wait_ge(bank_full, nth[e] + 1)
                    turned = bank(e).bitcast(BF16)[0:MAX_ROWS, :]
                    if a < SELF_A:
                        b, h = a // PAIRS, 2 * (a % PAIRS)
                        act.activation(ops[b][MAX_ROW:CROSS_ROWS, 0, h:h + 2, :],
                                       turned[:, 0:S].unsqueeze(1).broadcast_to([MAX_ROWS, 2, S]), ACT.Copy)\
                           .then_inc(act_emptied, 1)
                    else:
                        b, g = cross(a)
                        act.activation(of_group(qx[b], g),
                                       turned[:, 0:P].unsqueeze(1).broadcast_to([MAX_ROWS, HG, P]),
                                       ACT.Copy).then_inc(act_emptied, 1)
                elif kind == "O":
                    u = e[1]
                    act.wait_ge(c_done, u + 1)
                    if u >= 1:
                        act.wait_ge(bank_full, nth[("norm", u - 1)] + 1)
                    w = S if u < SELF_U else P
                    act.activation(outT[:, 0:w], psC[:, 0:w], ACT.Copy).then_inc(outT_ready, 1)
                elif kind in ON_ACT:
                    act.wait_ge(bank_full, nth[e] + 1)
                    bk_ = bank(e)
                    if kind == "xval":
                        _, b, i = e
                        for j in range(2):
                            ins = act.activation(v_cross[:, b, 2 * i + j, :, 0:HD],
                                                 bk_[:, j * D:j * D + D].rearrange("p (h d) -> p h d", h=H), ACT.Copy)
                    elif kind == "mean":
                        ins = act.activation(meanv[:, e[1], :], bk_[:, 0:D], ACT.Copy)
                    elif kind == "fr":
                        lo, hi = by_bank(e[2])[e[3]]
                        ins = act.activation(attn[:, e[1], lo:hi, :].rearrange("p q d -> p (q d)"),
                                             bk_[:, 0:(hi - lo) * D], ACT.Tanh, scale=0.5)
                    elif kind in ("x2T", "fk"):
                        _, b, part, c = e
                        lo, hi = PARTS[part]
                        if kind == "fk":
                            act.wait_ge(mix_done, 4 * mixB_no[("mixB", b, part)] + 4)
                        ins = act.activation(xT_sb[:, b, c, lo * P:hi * P], bk_[:, 0:(hi - lo) * P],
                                             ACT.Relu if kind == "fk" else ACT.Copy)
                    elif kind == "x1T":
                        ins = act.activation(xT_sb[:, e[1], :, LAST * P:S], bk_[:, 0:CC * P].rearrange(
                            "p (c t) -> p c t", c=CC), ACT.Copy)
                    else:
                        ins = act.activation(xT_sb[:, e[1], e[2], :], bk_, ACT.Copy)
                    ins.then_inc(act_emptied, 1)
                elif kind == "fill":
                    b = e[1]
                    act.wait_ge(bank_full, nth[("attnT", b, CC - 1)] + 1)
                    wait_emptied(act, ("mean", b))
                    act.activation(attn[:, b, :, :], meanv[:, b, :].unsqueeze(1).broadcast_to([P, QT, D]), ACT.Copy)\
                       .then_inc(filled, 1)
                elif kind == "mixA":
                    _, b, part = e
                    lo, hi = PARTS[part][0] * P, min(PARTS[part][1] * P, S - 1)
                    wait_emptied(act, ("x2T", b, part, CC - 1))
                    act.wait_ge(om_ready, 2)
                    for om, mixed in ((om_k, xk), (om_r, xr)):
                        for cc in range(CC):
                            act.activation(mixed[b][:, cc, lo + 1:hi + 1], xT_sb[:, b, cc, lo:hi], ACT.Copy,
                                           scale=om[:, cc:cc + 1]).then_inc(mix_prev, 1)
                elif kind == "rare":
                    b = e[1]
                    for t, at in rare_tiles(act, b):
                        act.wait_ge(X[b]["q_pe"], at("q_pe", 1))
                        act.activation(xT_sb[:, b, :, 0:P], psN[:, 0, 0:CC * P].rearrange("p (c t) -> p c t", c=CC),
                                       ACT.Copy).then_inc(X[b]["q_act"], 1)
                        for f in job:
                            if f[0] == "B":
                                _, g, i = f
                                act.wait_ge(X[b]["b_full"], at("b_full", 8 * g + i + 1))
                                if g >= 1 and i == 0:
                                    act.wait_ge(X[b]["c_done"], at("c_done", g))
                                act.activation(pcross[:, RARE, i // 2, 4 * (i % 2):4 * (i % 2) + 4, :]
                                               .rearrange("p k t -> p (k t)"), psB[:, i % 2, :], ACT.Exp)\
                                   .then_inc(X[b]["exp"], 1)
                            elif f[0] == "M":
                                g = f[1]
                                act.wait_ge(X[b]["turned"], at("turned", g + 1))
                                act.activation(of_group(qrare[b], g),
                                               turned_rare.unsqueeze(1).broadcast_to([MAX_ROWS, HG, P]),
                                               ACT.Copy).then_inc(X[b]["rows"], 1)
                            elif f[0] == "O":
                                g = f[1]
                                act.wait_ge(X[b]["c_done"], at("c_done", g + 1))
                                if g >= 1:
                                    act.wait_ge(X[b]["n_full"], at("n_full", g))
                                act.activation(outT[:, 0:P], psC[:, 0:P], ACT.Copy).then_inc(X[b]["outT"], 1)

        @block.vector
        def _(dve):
            steps = [0]

            def step(ins):
                steps[0] += 1
                ins.then_inc(dve_step, 1)
                dve.wait_ge(dve_step, steps[0])

            dve.memset(warm, 0.0).then_inc(warm_ready, 1)
            dve.memset(psC[:, :], 0.0).then_inc(init_done, 1)
            for at_e, e in enumerate(order):
                kind = e[0]
                if e == ("A", 0, 0):
                    for q in range(QT):
                        ins = dve.memset(weight[0:1, :, q:q + 1], float(QT - 1 - q))
                    dve.wait_ge(in_mask, 32)
                    step(dve.tensor_reduce(live[0:1, :, :], mask_row[0:1, :, :, :], AX, ALU.max))
                    step(dve.tensor_tensor(live[0:1, :, :], live[0:1, :, :], weight[0:1, :, :], ALU.mult))
                    step(dve.tensor_reduce(behind[0:1, :], live[0:1, :, :].rearrange("p b q -> p (b q)"), AX, ALU.max))
                    dve.tensor_scalar(count_i[0:1, :], behind[0:1, :], 0.0, None, ALU.add).then_inc(count_ready, 1)
                    dve.wait_ge(in_qk, 16 * 3)
                    dve.tensor_scalar(om_r[:, :], mur_c, -1.0, 1.0, ALU.mult, ALU.add).then_inc(om_ready, 1)
                    dve.tensor_scalar(om_k[:, :], muk_c, -1.0, 1.0, ALU.mult, ALU.add).then_inc(om_ready, 1)
                if e == ("A", 0, 0):
                    load_count(dve)
                if kind == "A":
                    _, a, i = e
                    n = 8 * a + i
                    if i == 0 and a >= 2:
                        dve.wait_ge(max_parts, a - 1)
                    dve.wait_ge(a_full, n + 1)
                    dve.tensor_reduce(mx[:, a % 2, i:i + 1], psA[:, n % 3, :], AX, ALU.max).then_inc(a_max, 1)
                elif kind == "chain":
                    a = e[1]
                    m = mx[:, a % 2, :].rearrange("p (j q) -> p j q", j=2 if a < SELF_A else HG)
                    dve.wait_ge(a_max, 8 * (a + 1))
                    if a < 2:
                        dve.wait_ge(init_done, INIT)
                    else:
                        dve.wait_ge(bank_full, nth[("M", a - 2)] + 1)
                    if a < SELF_A:
                        j = 2 * (a % 2)
                        o = [mparts[:, a % 2, :, j:j + 2, part].rearrange("p q j -> p j q") for part in range(2)]
                    else:
                        dve.wait_ge(max_parts, a)
                        step(dve.tensor_reduce(cmax[:, :], m, AX, ALU.max))
                        m = cmax[:, :]
                        o = [mparts[:, a % 2, 0, :, part] for part in range(2)]
                    step(dve.tensor_scalar(o[0], m, -1.0, None, ALU.mult))
                    dve.scalar_tensor_tensor(out=o[1], in0=m, scalar=-1.0, in1=o[0], op0=ALU.mult, op1=ALU.subtract)\
                       .then_inc(max_parts, 1)
                elif kind == "ctxsum":
                    b = e[1]
                    dve.wait_ge(in_ctx, 16 * (2 + b))
                    step(dve.tensor_reduce(csum[:, :], ctx_sb[0:XC, :, :], AX, ALU.add))
                    if b:
                        dve.wait_ge(bank_full, nth[("mean", 0)] + 1)
                    dve.tensor_scalar(csum_r[:, :, :], csum[:, :].unsqueeze(2).broadcast_to([XC, 2, P]), 1.0 / S2,
                                      None, ALU.mult).then_inc(csum_ready, 1)
                elif kind == "fk" and e[2] == 1:
                    square(dve, e)
                elif kind in ("proj", "val", "norm", "wo", "fv"):
                    dve.wait_ge(bank_full, nth[e] + 1)
                    bk_ = bank(e)
                    if kind == "proj":
                        _, w, b, dc, half = e
                        k = split_no[e]
                        if k >= 2:
                            wait_split(dve, splits[k - 2])
                        v, pt, bk_ = q32[:, k % 2, 0:width(w)], parts[:, k % 2, :, 0:width(w)], bk_[:, 0:width(w)]
                        if w == "q":
                            ins = dve.tensor_scalar(v, bk_, bq_c[:, dc:dc + 1], QSCALE, ALU.add, ALU.mult)
                        elif w == "k":
                            ins = dve.tensor_scalar(v, bk_, bk_c[:, dc:dc + 1], None, ALU.add)
                        else:
                            ins = dve.tensor_scalar(v, bk_, QSCALE if w == "c" else 1.0, None, ALU.mult)
                        ins.then_inc(dve_emptied, 1)
                        if fast(e):
                            dve.wait_ge(dve_emptied, rank[e])
                            if k >= 2:
                                wait_written(dve, k - 2)
                            step(dve.tensor_copy(pt[:, 0, :], v))
                            step(dve.tensor_tensor(v, v, pt[:, 0, :], ALU.subtract))
                            step(dve.tensor_copy(pt[:, 1, :], v))
                            dve.tensor_tensor(pt[:, 2, :], v, pt[:, 1, :], ALU.subtract).then_inc(dve_split, 1)
                    elif kind == "val":
                        _, b, half = e
                        dve.wait_ge(in_v, 16 * 3)
                        for j in range(2):
                            ins = dve.tensor_tensor(vs[:, b, 2 * half + j, :, 0:HD],
                                                    bk_[:, j * D:j * D + D].rearrange("p (h d) -> p h d", h=H),
                                                    bv_r[:, :].rearrange("p (h d) -> p h d", h=H), ALU.add)
                        ins.then_inc(dve_emptied, 1)
                    elif kind == "norm":
                        u = e[1]
                        tiles = QT if u < SELF_U else 1
                        b, g = u % SELF_U // UNITS, u % UNITS
                        turned = bk_.rearrange("p (q j c) -> p q j c", q=QT, j=HG)
                        if u:
                            wait_emptied(dve, ("norm", u - 1))
                        step(dve.reciprocal(rden[:, 0:tiles, :], turned[:, 0:tiles, :, HD]))
                        for q in range(tiles):
                            dst = attn[:, b, q, :] if u < SELF_U else tile_att[:, b, :]
                            ins = dve.tensor_tensor(
                                dst[:, 64 * g:64 * g + 64].rearrange("p (j d) -> p j d", j=HG),
                                turned[:, q, :, 0:HD], rden[:, q, :].unsqueeze(2).broadcast_to([P, HG, HD]), ALU.mult)
                        ins.then_inc(dve_emptied, 1)
                    elif kind == "wo":
                        _, b, half = e
                        dve.wait_ge(residual, b + 1)
                        r = x_sb[:, b, 2 * half:2 * half + 2, :].rearrange("p q d -> p (q d)")
                        dve.tensor_tensor(r, bk_, r, ALU.add).then_inc(dve_emptied, 1)
                    else:
                        _, b, part, n = e
                        lo, hi = by_bank(part)[n]
                        wait_emptied(dve, ("fr",) + e[1:])
                        gated = attn[:, b, lo:hi, :].rearrange("p q d -> p (q d)")
                        dve.scalar_tensor_tensor(out=gated, in0=gated, scalar=1.0, in1=bk_[:, 0:(hi - lo) * D],
                                                 op0=ALU.add, op1=ALU.mult).then_inc(dve_emptied, 1)
                        wait_emptied(dve, e)
                        r = x_sb[:, b, lo:hi, :].rearrange("p q d -> p (q d)")
                        step(dve.scalar_tensor_tensor(out=r, in0=gated, scalar=0.5, in1=r, op0=ALU.mult, op1=ALU.add))
                elif kind == "lnA":
                    _, which, b, part = e
                    n, (lo, hi) = ln_no[e[1:]], PARTS[part]
                    if which == 1:
                        wait_emptied(dve, ("wo", b, 1 if part == 1 else 0))
                    if which == 2 and part == 0:
                        dve.wait_ge(summed, b + 1)
                    if which == 2 and part == 1:
                        dve.wait_ge(filled, b + 1)
                        step(dve.tensor_tensor(x_sb[:, b, lo:hi, :], x_sb[:, b, lo:hi, :], attn[:, b, lo:hi, :], ALU.add))
                    if n > 1:
                        dve.wait_ge(ln_done, n - 1)
                    for q in range(lo, hi):
                        ins = dve.bn_stats(stats[:, q, :], x_sb[:, b, q, :])
                    step(ins)
                    for q in range(lo, hi):
                        ins = dve.bn_aggr(mv[:, q, :], stats[:, q, :])
                    step(ins)
                    dve.tensor_scalar(ve[:, lo:hi], mv[:, lo:hi, 1], EPS, None, ALU.add).then_inc(var_ready, 1)
                elif kind == "lnB":
                    _, which, b, part = e
                    lo, hi = PARTS[part]
                    dve.wait_ge(rstd_ready, ln_no[e[1:]])
                    for q in range(lo, hi):
                        ins = dve.tensor_scalar(x_sb[:, b, q, :], x_sb[:, b, q, :], mv[:, q, 0:1], rstd[:, q:q + 1],
                                                ALU.subtract, ALU.mult)
                    ins.then_inc(ln_done, 1)
                elif kind == "select":
                    b = e[1]
                    dve.wait_ge(filled, b + 1)
                    wait_emptied(dve, ("norm", SELF_U + UNITS * b + UNITS - 1))
                    step(dve.copy_predicated(attn[:, b, LAST, :], mask_q[:, b, LAST:QT].broadcast_to([P, D]),
                                             tile_att[:, b, :]))
                elif kind == "mixB":
                    _, b, part = e
                    lo, hi = PARTS[part][0] * P, PARTS[part][1] * P
                    mixes = ((muk_c, xk), (mur_c, xr))
                    if part == 0:
                        for mu, mixed in mixes:
                            dve.memset(mixed[b][:, :, 0:1], 0.0).then_inc(first_ready, 1)
                        dve.wait_ge(first_ready, 2 * (b + 1))
                    for m, (mu, mixed) in enumerate(mixes):
                        for cc in range(CC):
                            dve.wait_ge(mix_prev, 4 * mixB_no[e] + 2 * m + cc + 1)
                            dve.scalar_tensor_tensor(out=mixed[b][:, cc, lo:hi], in0=xT_sb[:, b, cc, lo:hi],
                                                     scalar=mu[:, cc:cc + 1], in1=mixed[b][:, cc, lo:hi],
                                                     op0=ALU.mult, op1=ALU.add).then_inc(mix_done, 1)
                elif kind == "rare":
                    b = e[1]

                    def settle():
                        done = order[:at_e]

                        def count(k):
                            return sum(1 for f in done if f[0] == k)
                        for k in [k for f, k in split_no.items() if f in done][-2:]:
                            wait_split(dve, splits[k])
                            wait_written(dve, k)
                        for s, n in ((a_max, count("A")), (exp_done, count("B")), (ln_done, count("lnB")),
                                     (outT_ready, count("O")), (c_done, count("O")), (filled, b + 1),
                                     (act_emptied, sum(1 for f in done if f[0] in ON_ACT)),
                                     (dve_emptied, sum(1 for f in done if f in nth and f[0] not in ON_ACT))):
                            dve.wait_ge(s, n)
                        dve.memset(gate_pad[:, :], 0.0).then_inc(gate[b], 1)

                    for t, at in rare_tiles(dve, b, settle):
                        dve.tensor_copy(tile_sel, x_sb[:, b, bass.ts(t, 1), :].rearrange("p a d -> p (a d)"))\
                           .then_inc(X[b]["q_dve"], 1)
                        dve.wait_ge(X[b]["q_pe"], at("q_pe", 2))
                        dve.memset(gate_pad[:, :], 0.0)
                        v, pt = q32[:, 0, 0:CC * P], parts[:, 0, :, 0:CC * P]
                        dve.tensor_scalar(v, psN[:, 1, 0:CC * P], QSCALE, None, ALU.mult).then_inc(X[b]["q_dve"], 1)
                        dve.wait_ge(X[b]["q_dve"], at("q_dve", 2))
                        dve.tensor_copy(pt[:, 0, :], v).then_inc(X[b]["q_dve"], 1)
                        dve.wait_ge(X[b]["q_dve"], at("q_dve", 3))
                        dve.tensor_tensor(v, v, pt[:, 0, :], ALU.subtract).then_inc(X[b]["q_dve"], 1)
                        dve.wait_ge(X[b]["q_dve"], at("q_dve", 4))
                        dve.tensor_copy(pt[:, 1, :], v).then_inc(X[b]["q_dve"], 1)
                        dve.wait_ge(X[b]["q_dve"], at("q_dve", 5))
                        dve.tensor_tensor(pt[:, 2, :], v, pt[:, 1, :], ALU.subtract).then_inc(X[b]["q_dve"], 1)
                        for f in job:
                            if f[0] == "A":
                                _, g, i = f
                                if i == 0 and g >= 1:
                                    dve.wait_ge(X[b]["max2"], at("max2", g))
                                dve.wait_ge(X[b]["a_full"], at("a_full", 8 * g + i + 1))
                                dve.tensor_reduce(xm[:, i // 2, i % 2:i % 2 + 1], psA[:, i % 2, :], AX, ALU.max)\
                                   .then_inc(X[b]["a_max"], 1)
                                if i == 7:
                                    dve.wait_ge(X[b]["a_max"], at("a_max", 8 * (g + 1)))
                                    if g >= 1:
                                        dve.wait_ge(X[b]["parts"], at("parts", 3 * g))
                                    dve.tensor_reduce(xmax[:, :], xm[:, :, :], AX, ALU.max).then_inc(X[b]["max2"], 1)
                            elif f[0] == "norm":
                                g = f[1]
                                dve.wait_ge(X[b]["n_full"], at("n_full", g + 1))
                                turned = psN[:, g % 2, 0:P].rearrange("p (j c) -> p j c", j=HG)
                                if g:
                                    dve.wait_ge(X[b]["n_done"], at("n_done", 2 * g))
                                dve.reciprocal(xrd[:, :], turned[:, :, HD]).then_inc(X[b]["n_done"], 1)
                                dve.wait_ge(X[b]["n_done"], at("n_done", 2 * g + 1))
                                dve.tensor_tensor(tile_rare[:, 64 * g:64 * g + 64].rearrange("p (j d) -> p j d", j=HG),
                                                  turned[:, :, 0:HD], xrd[:, :].unsqueeze(2).broadcast_to([P, HG, HD]),
                                                  ALU.mult).then_inc(X[b]["n_done"], 1)
                        dve.wait_ge(X[b]["n_done"], at("n_done", 2 * UNITS))
                        dve.memset(gate_pad[:, :], 0.0)
                        dve.tensor_copy(mcur[:, :], mask_q[:, b, bass.ts(t, 1)]).then_inc(X[b]["n_done"], 1)
                        dve.tensor_copy(tile_sel, meanv[:, b, :]).then_inc(X[b]["n_done"], 1)
                        dve.wait_ge(X[b]["n_done"], at("n_done", 2 * UNITS + 2))
                        dve.memset(gate_pad[:, :], 0.0)
                        dve.copy_predicated(tile_sel, mcur[:, :].broadcast_to([P, D]), tile_rare)\
                           .then_inc(X[b]["n_done"], 1)
                        dve.wait_ge(X[b]["n_done"], at("n_done", 2 * UNITS + 3))
                        dve.tensor_copy(attn[:, b, bass.ts(t, 1), :].rearrange("p a d -> p (a d)"), tile_sel)\
                           .then_inc(gate[b], 1)

        @block.tensor
        def _(pe):
            def project(e, terms):
                bk_ = bank(e)
                for c0, c1, pairs in terms:
                    for n, (l, r) in enumerate(pairs):
                        ins = pe.matmul(bk_[:, c0:c1], l, r, start=(n == 0), stop=(n == len(pairs) - 1))
                ins.then_inc(bank_full, 1)

            def by_tile(e, lo, hi, source, w):
                project(e, [(j * D, j * D + D, [(source(c, slice((lo + j) * P, (lo + j + 1) * P)), w[:, c, :])
                                                for c in range(CC)]) for j in range(hi - lo)])

            def turn(e, sources):
                bk_ = bank(e)
                for q, src in enumerate(sources):
                    ins = pe.transpose(bk_[:, q * P:q * P + P], src, identf[:, :])
                ins.then_inc(bank_full, 1)

            def rare_ready(b):
                pe.wait_ge(kx_in[b], 16 * 2 * CC)
                wait_emptied(pe, ("xval", b, XKB // 2 - 1))

            pe.wait_ge(warm_ready, 1)
            for n in range(WARM_UP):
                pe.matmul(psB[:, n % 2, :], warm[:, 0:P], warm, start=True, stop=True)
            for e in order:
                kind = e[0]
                if e == ("A", 0, 0):
                    load_count(pe)
                if e in nth and nth[e] >= 2:
                    wait_emptied(pe, items[nth[e] - 2])
                if kind == "proj":
                    _, w, b, dc, half = e
                    if w == "x":
                        pe.wait_ge(in_ctx, 16 * (2 + b))
                        project(e, [(0, S, [(w_kv[:, c, dc * P:dc * P + P], ctx_sb[0:XC, c, half * S:half * S + S])
                                            for c in range(2)])])
                        continue
                    if w == "c":
                        pe.wait_ge(in_late, 16 * 5)
                        wait_emptied(pe, ("x1T", b))
                        project(e, [(d * P, d * P + P, [(w_xq[:, c, d * P:d * P + P], xT_sb[:, b, c, LAST * P:S])
                                                        for c in range(CC)]) for d in range(CC)])
                        continue
                    else:
                        pe.wait_ge(in_qk, 16 * 3)
                        if b:
                            pe.wait_ge(in_v, 16 * 3)
                        wt = w_qk[:, :, 0:D] if w == "q" else w_qk[:, :, D:2 * D]
                    project(e, [(0, S, [(wt[:, c, dc * P:dc * P + P], xT_sb[:, b, c, :]) for c in range(CC)])])
                elif kind == "val":
                    pe.wait_ge(in_v, 16 * 3)
                    by_tile(e, 2 * e[2], 2 * e[2] + 2, lambda c, t: xT_sb[:, e[1], c, t], w_v)
                elif kind == "xval":
                    _, b, i = e
                    pe.wait_ge(in_ctx, 16 * (2 + b))
                    project(e, [(j * D, j * D + D, [(ctx_sb[0:XC, c, (2 * i + j) * P:(2 * i + j + 1) * P],
                                                     w_kv[:, c, D:2 * D]) for c in range(2)]) for j in range(2)])
                elif kind == "mean":
                    pe.wait_ge(csum_ready, e[1] + 1)
                    project(e, [(0, D, [(csum_r[:, c, :], w_kv[:, c, D:2 * D]) for c in range(2)])])
                elif kind == "norm":
                    u = e[1]
                    pe.wait_ge(outT_ready, u + 1)
                    turn(e, [outT[:, q * P:q * P + P] for q in range(QT if u < SELF_U else 1)])
                elif kind == "attnT":
                    _, b, dc = e
                    wait_emptied(pe, ("norm", UNITS * b + UNITS - 1))
                    turn(e, [attn[:, b, q, dc * P:dc * P + P] for q in range(QT)])
                elif kind == "wo":
                    pe.wait_ge(in_late, 16 * 5)
                    wait_emptied(pe, ("attnT", e[1], CC - 1))
                    by_tile(e, 2 * e[2], 2 * e[2] + 2, lambda c, t: xT_sb[:, e[1], c, t], w_o)
                elif kind == "x1T":
                    b = e[1]
                    pe.wait_ge(ln_done, ln_no[(1, b, 1)])
                    turn(e, [x_sb[:, b, LAST, c * P:c * P + P] for c in range(CC)])
                elif kind == "x2T":
                    _, b, part, cc = e
                    pe.wait_ge(ln_done, ln_no[(2, b, part)])
                    turn(e, [x_sb[:, b, q, cc * P:cc * P + P] for q in range(*PARTS[part])])
                elif kind == "fk":
                    _, b, part, dc = e
                    lo, hi = PARTS[part]
                    pe.wait_ge(in_ffn, 16 * 3)
                    pe.wait_ge(mix_done, 4 * mixB_no[("mixB", b, part)] + 2)
                    project(e, [(0, (hi - lo) * P, [(w_k2[:, c, dc * P:dc * P + P], xk[b][:, c, lo * P:hi * P])
                                                    for c in range(CC)])])
                elif kind == "fr":
                    _, b, part, n = e
                    pe.wait_ge(mix_done, 4 * mixB_no[("mixB", b, part)] + 4)
                    by_tile(e, *by_bank(part)[n], lambda c, t: xr[b][:, c, t], w_r)
                elif kind == "fv":
                    _, b, part, n = e
                    pe.wait_ge(squared[part], fk_no[("fk", b, part, CC - 1)])
                    by_tile(e, *by_bank(part)[n], lambda c, t: xT_sb[:, b, c, t], w_v2)
                elif kind == "A":
                    _, a, i = e
                    n = 8 * a + i
                    if n >= 3:
                        pe.wait_ge(a_max, n - 2)
                    if a < SELF_A:
                        b, h, q = a // PAIRS, 2 * (a % PAIRS) + i // 4, i % 4
                        if i == 0 and a % 4 == 0:
                            pe.wait_ge(rows_in[b][(a % PAIRS) // 4], 16 * 2)
                            pe.wait_ge(in_const[b], 16 * 2)
                        rows, keys = ops[b][0:SELF_ROWS, 0, h, q * P:q * P + P], ops[b][0:SELF_ROWS, 1, h, :]
                    else:
                        b, g = cross(a)
                        h, half = HG * g + i // 2, i % 2
                        if i == 0 and g == 0:
                            pe.wait_ge(kx_in[b], 16 * 2 * CC)
                            pe.wait_ge(qx_in[b], 16)
                        rows, keys = of_head(qx[b], SPLIT_ROWS, h), kx[b][0:SPLIT_ROWS, h, half * S:half * S + S]
                    pe.matmul(psA[:, n % 3, :], rows, keys, start=True, stop=True).then_inc(a_full, 1)
                elif kind == "M":
                    a = e[1]
                    pe.wait_ge(init_done, INIT)
                    pe.wait_ge(max_parts, a + 1)
                    for q in range(QT if a < SELF_A else 1):
                        ins = pe.transpose(bank(e).bitcast(BF16)[0:MAX_ROWS, q * P:q * P + P],
                                           mparts[:, a % 2, q, :, :].rearrange("p j c -> p (j c)"), identb[:, :])
                    ins.then_inc(bank_full, 1)
                elif kind == "B":
                    _, a, i = e
                    n = 8 * a + i
                    if i == 0:
                        wait_emptied(pe, ("M", a))
                    if n >= 2:
                        pe.wait_ge(exp_done, n - 1)
                    if a < SELF_A:
                        b, h, kb = a // PAIRS, 2 * (a % PAIRS) + i // 4, i % 4
                        ins = pe.matmul(psB[:, n % 2, :], ops[b][0:SELF_ROWS, 1, h, kb * P:kb * P + P],
                                        ops[b][0:SELF_ROWS, 0, h, :], start=True, stop=True)
                    else:
                        b, g = cross(a)
                        h = HG * g + i // 2
                        for k in range(4):
                            kb = 4 * (i % 2) + k
                            ins = pe.matmul(psB[:, n % 2, k * P:k * P + P], kx[b][0:CROSS_ROWS, h, kb * P:kb * P + P],
                                            of_head(qx[b], CROSS_ROWS, h), start=True, stop=True)
                    ins.then_inc(b_full, 1)
                elif kind == "C":
                    _, u, kb = e
                    b, g = u % SELF_U // UNITS, u % UNITS
                    if kb == 0:
                        pe.wait_ge(exp_done, 16 * (u + 1) if u < SELF_U else 8 * (u - SELF_U + SELF_A + 1))
                        pe.wait_ge(init_done, INIT)
                        if u:
                            pe.wait_ge(outT_ready, u)
                        if g == 0:
                            wait_emptied(pe, ("val", b, 1) if u < SELF_U else ("xval", b, XKB // 2 - 1))
                    blocks = KB if u < SELF_U else XKB
                    for j in range(HG):
                        if u < SELF_U:
                            vals, exps, w = vs[:, b, kb, HG * g + j, :], pself[:, (HG * u + j) % PRING, kb, :], S
                        else:
                            vals, exps, w = v_cross[:, b, kb, HG * g + j, :], pcross[:, (u + 1) % 2, j, kb, :], P
                        ins = pe.matmul(psC[32 * j:32 * j + VW, 0:w], vals, exps, start=(kb == 0),
                                        stop=(kb == blocks - 1))
                    if kb == blocks - 1:
                        ins.then_inc(c_done, 1)
                elif kind == "rare":
                    b = e[1]
                    for t, at in rare_tiles(pe, b, lambda: rare_ready(b)):
                        pe.wait_ge(X[b]["q_dve"], at("q_dve", 1))
                        for c in range(CC):
                            ins = pe.transpose(psN[:, 0, c * P:c * P + P], tile_sel[:, c * P:c * P + P], identf[:, :])
                        ins.then_inc(X[b]["q_pe"], 1)
                        pe.wait_ge(X[b]["q_act"], at("q_act", 1))
                        for d in range(CC):
                            for c in range(CC):
                                ins = pe.matmul(psN[:, 1, d * P:d * P + P], w_xq[:, c, d * P:d * P + P],
                                                xT_sb[:, b, c, 0:P], start=(c == 0), stop=(c == CC - 1))
                        ins.then_inc(X[b]["q_pe"], 1)
                        for f in job:
                            if f[0] == "A":
                                _, g, i = f
                                if g == 0 and i == 0:
                                    pe.wait_ge(qrare_in[b], at("qx", 16))
                                if 8 * g + i >= 2:
                                    pe.wait_ge(X[b]["a_max"], at("a_max", 8 * g + i - 1))
                                h = HG * g + i // 2
                                pe.matmul(psA[:, i % 2, :], of_head(qrare[b], SPLIT_ROWS, h),
                                          kx[b][0:SPLIT_ROWS, h, (i % 2) * S:(i % 2) * S + S], start=True, stop=True)\
                                  .then_inc(X[b]["a_full"], 1)
                            elif f[0] == "M":
                                g = f[1]
                                pe.wait_ge(X[b]["parts"], at("parts", 3 * (g + 1)))
                                if g:
                                    pe.wait_ge(X[b]["rows"], at("rows", g))
                                pe.transpose(turned_rare, xparts[:, :, :].rearrange("p j c -> p (j c)"),
                                             identb[:, :]).then_inc(X[b]["turned"], 1)
                            elif f[0] == "B":
                                _, g, i = f
                                if i == 0:
                                    pe.wait_ge(X[b]["rows"], at("rows", g + 1))
                                if 8 * g + i >= 2:
                                    pe.wait_ge(X[b]["exp"], at("exp", 8 * g + i - 1))
                                h = HG * g + i // 2
                                for k in range(4):
                                    kb = 4 * (i % 2) + k
                                    ins = pe.matmul(psB[:, i % 2, k * P:k * P + P],
                                                    kx[b][0:CROSS_ROWS, h, kb * P:kb * P + P],
                                                    of_head(qrare[b], CROSS_ROWS, h), start=True, stop=True)
                                ins.then_inc(X[b]["b_full"], 1)
                            elif f[0] == "C":
                                _, g, kb = f
                                if kb == 0:
                                    pe.wait_ge(X[b]["exp"], at("exp", 8 * (g + 1)))
                                    if g:
                                        pe.wait_ge(X[b]["outT"], at("outT", g))
                                for j in range(HG):
                                    ins = pe.matmul(psC[32 * j:32 * j + VW, 0:P], v_cross[:, b, kb, HG * g + j, :],
                                                    pcross[:, RARE, j, kb, :], start=(kb == 0), stop=(kb == XKB - 1))
                                if kb == XKB - 1:
                                    ins.then_inc(X[b]["c_done"], 1)
                            elif f[0] == "norm":
                                g = f[1]
                                pe.wait_ge(X[b]["outT"], at("outT", g + 1))
                                if g >= 2:
                                    pe.wait_ge(X[b]["n_done"], at("n_done", 2 * (g - 1)))
                                pe.transpose(psN[:, g % 2, 0:P], outT[:, 0:P], identf[:, :])\
                                  .then_inc(X[b]["n_full"], 1)


def kernel(**inputs):
    import ml_dtypes
    import numpy as np
    import concourse.bacc as bacc
    from concourse.bass_utils import run_bass_kernel_spmd as run

    def arr(name):
        return np.asarray(inputs[name])

    def by_head(b):
        return np.ascontiguousarray(b.reshape(CC, H // CC, HD).transpose(2, 1, 0).reshape(P, CC))

    def columns(w):
        return np.ascontiguousarray(w.reshape(-1, CC, H // CC, HD).transpose(0, 1, 3, 2).reshape(-1, D))

    def T(a):
        return np.ascontiguousarray(np.swapaxes(a, -1, -2))

    slopes = (np.float32(1) / np.float32(2) ** (np.arange(H, dtype=np.float32) / np.float32(H))).astype(np.float32)
    term = slopes[:, None] * np.arange(S, dtype=np.float32)[None, :]
    hi = term.astype(ml_dtypes.bfloat16)
    mid = (term - hi.astype(np.float32)).astype(ml_dtypes.bfloat16)
    low = (term - hi.astype(np.float32) - mid.astype(np.float32)).astype(ml_dtypes.bfloat16)
    one = np.ones_like(hi)
    mine = [one * (np.arange(H) % HG == r // 2).astype(ml_dtypes.bfloat16)[:, None] for r in range(MAX_ROWS)]
    k_rows = np.stack(mine + [hi, mid, low])
    q_rows = np.stack([0 * one] * MAX_ROWS + [one, one, one])
    kvT = T(arr("L0_xattn_Wkv"))
    data = {
        "x": arr("x"), "xT": T(arr("x")), "ctxT": T(arr("ctx_768")), "mask": arr("mask_BxS_bk0"),
        "w_qk": np.concatenate([columns(arr("L0_attn_Wq")), columns(arr("L0_attn_Wk"))], axis=1),
        "cols": np.concatenate([by_head(arr("L0_attn_bq")), by_head(arr("L0_attn_bk")), T(arr("L0_ffn_mu_r").reshape(CC, P)),
                                T(arr("L0_ffn_mu_k").reshape(CC, P))], axis=1),
        "wv": arr("L0_attn_Wv"), "bv": arr("L0_attn_bv"), "wo": arr("L0_attn_Wo"),
        "bo": arr("L0_attn_bo"), "xwqT": columns(T(arr("L0_xattn_Wq"))),
        "xwkvT": np.concatenate([columns(kvT[:, :D]), kvT[:, D:]], axis=1),
        "wrT": T(arr("L0_ffn_W_r")), "wkT": T(arr("L0_ffn_W_k")), "wvT": T(arr("L0_ffn_W_v")),
        "k_rows": k_rows, "q_rows": q_rows, "ident": np.eye(P, dtype=np.float32),
    }
    nc = bacc.Bacc("TRN2", target_bir_lowering=False, num_devices=1)
    arrays, args = {}, []
    for name, a in data.items():
        a = np.ascontiguousarray(a)
        arrays[f"in_{name}"] = a
        args.append(nc.dram_tensor(f"in_{name}", a.shape, mybir.dt.from_np(a.dtype), kind="ExternalInput").ap())
    args.append(nc.dram_tensor("out_x", (B, S, D), F32, kind="ExternalOutput").ap())
    decoder_layer(nc, *args)
    return run(nc, [arrays], core_ids=[0]).results[0]["out_x"]
```
